# Optimizing a Trainium2 kernel written in Bass

```python
import numpy as np
import jax
import jax.numpy as jnp

def _softmax(x, axis=-1):
    return jax.nn.softmax(x, axis=axis)

def _gelu(x):
    return jax.nn.gelu(x, approximate=True)

def _silu(x):
    return jax.nn.silu(x)

def _sigmoid(x):
    return jax.nn.sigmoid(x)

def _layernorm(x, axis=-1, eps=1e-05):
    m = jnp.mean(x, axis=axis, keepdims=True)
    v = jnp.var(x, axis=axis, keepdims=True)
    return (x - m) / jnp.sqrt(v + eps)

def _scatter_add(tgt, idx, src, axis=0):
    return tgt.at[idx].add(src)

def _segment_sum(src, seg, n):
    return jax.ops.segment_sum(src, seg, n)
kernel_name = 'mk_flamingo_gated_d1_seqx_r4_aeed24'

def setup_inputs(seed: int=0):
    np.random.seed(seed)
    _w = jnp.asarray

    def _rec_inputs():
        import jax
        import jax.numpy as jnp
        _rk = jax.random.key(seed)
        x = -0.0002928 + 1 * jax.random.normal(jax.random.fold_in(_rk, 1), (16, 256, 256), jnp.float32)
        _lenS = 256 - jax.random.randint(jax.random.fold_in(_rk, 7), (16,), 0, max(1, 256 // 4) + 1, jnp.int32)
        _lenS2 = 256 - jax.random.randint(jax.random.fold_in(_rk, 8), (16,), 0, max(1, 256 // 4) + 1, jnp.int32)
        _ctx_1024P = jax.random.normal(jax.random.fold_in(_rk, 11), (16, 16, 256), jnp.float32)
        _ctx_1024c = jax.random.dirichlet(jax.random.fold_in(_rk, 511), 0.3 * jnp.ones((16,), jnp.float32), (16, 256))
        _ctx_1024t = jnp.einsum('bsk,bkd->bsd', _ctx_1024c, _ctx_1024P)
        _ctx_1024t = _ctx_1024t * jax.lax.rsqrt(jnp.mean(jnp.square(_ctx_1024t)) + 1e-12) * 0.953939
        ctx_1024 = -1.39393e-06 + 0.999914 * (_ctx_1024t + 0.3 * jax.random.normal(jax.random.fold_in(_rk, 611), (16, 256, 256), jnp.float32))
        _g = jax.random.normal(jax.random.fold_in(_rk, 9001), (2, 1), jnp.float32)
        _g = jnp.sign(_g) * jnp.maximum(jnp.abs(_g), 1.0) + (_g == 0) * 1.0
        g_xattn = _g[0]
        g_ffn = _g[1]
        return (x, ctx_1024, g_xattn, g_ffn)
    x, ctx_1024, g_xattn, g_ffn = _rec_inputs()

    def _L0_xattn_setup():
        import jax, jax.numpy as jnp
        import numpy as np
        D_MODEL = 256
        N_HEADS = 16
        D_K = D_MODEL // N_HEADS
        key = jax.random.key(seed)
        ks = jax.random.split(key, 11)
        B, S = (2, 512)
        scale = 0.02
        inp = {'q': jax.random.normal(ks[0], (B, S, D_MODEL), jnp.float32), 'k': jax.random.normal(ks[1], (B, S, D_MODEL), jnp.float32), 'v': jax.random.normal(ks[2], (B, S, D_MODEL), jnp.float32), 'w_q': jax.random.normal(ks[3], (D_MODEL, D_MODEL), jnp.float32) * scale, 'b_q': jnp.zeros((D_MODEL,), jnp.float32), 'w_k': jax.random.normal(ks[4], (D_MODEL, D_MODEL), jnp.float32) * scale, 'b_k': jnp.zeros((D_MODEL,), jnp.float32), 'w_v': jax.random.normal(ks[5], (D_MODEL, D_MODEL), jnp.float32) * scale, 'b_v': jnp.zeros((D_MODEL,), jnp.float32), 'w_o': jax.random.normal(ks[6], (D_MODEL, D_MODEL), jnp.float32) * scale, 'b_o': jnp.zeros((D_MODEL,), jnp.float32)}
        return inp
    _L0_xattn_all = _L0_xattn_setup()
    _L0_xattn_in = {k: v for k, v in _L0_xattn_all.items() if k in ('w_q', 'b_q', 'w_k', 'b_k', 'w_v', 'b_v', 'w_o', 'b_o')}
    del _L0_xattn_all

    def _L0_ffn_setup():
        import jax, jax.numpy as jnp
        import numpy as np
        E, K = (8, 2)
        key = jax.random.key(seed)
        ks = jax.random.split(key, 5)
        B, S, H, I = (2, 256, 256, 1024)
        scale_h = 1.0 / np.sqrt(H)
        scale_i = 1.0 / np.sqrt(I)
        return {'hidden_states': jax.random.normal(ks[0], (B, S, H), jnp.float32), 'conf_w': jax.random.normal(ks[1], (E, H), jnp.float32) * 0.1 * scale_h, 'conf_b': jnp.zeros((E,), jnp.float32), 'gate_w': jax.random.normal(ks[2], (E, I, H), jnp.float32) * scale_h, 'up_w': jax.random.normal(ks[3], (E, I, H), jnp.float32) * scale_h, 'down_w': jax.random.normal(ks[4], (E, H, I), jnp.float32) * scale_i, 'wealth': jnp.ones((E,), jnp.float32)}
    _L0_ffn_all = _L0_ffn_setup()
    _L0_ffn_in = {k: v for k, v in _L0_ffn_all.items() if k in ('conf_w', 'conf_b', 'gate_w', 'up_w', 'down_w', 'wealth')}
    del _L0_ffn_all
    return {'x': x, 'ctx_1024': ctx_1024, 'g_xattn': g_xattn, 'g_ffn': g_ffn, 'L0_xattn_w_q': _L0_xattn_in['w_q'], 'L0_xattn_b_q': _L0_xattn_in['b_q'], 'L0_xattn_w_k': _L0_xattn_in['w_k'], 'L0_xattn_b_k': _L0_xattn_in['b_k'], 'L0_xattn_w_v': _L0_xattn_in['w_v'], 'L0_xattn_b_v': _L0_xattn_in['b_v'], 'L0_xattn_w_o': _L0_xattn_in['w_o'], 'L0_xattn_b_o': _L0_xattn_in['b_o'], 'L0_ffn_conf_w': _L0_ffn_in['conf_w'], 'L0_ffn_conf_b': _L0_ffn_in['conf_b'], 'L0_ffn_gate_w': _L0_ffn_in['gate_w'], 'L0_ffn_up_w': _L0_ffn_in['up_w'], 'L0_ffn_down_w': _L0_ffn_in['down_w'], 'L0_ffn_wealth': _L0_ffn_in['wealth']}

def reference(x, ctx_1024, g_xattn, g_ffn, L0_xattn_w_q, L0_xattn_b_q, L0_xattn_w_k, L0_xattn_b_k, L0_xattn_w_v, L0_xattn_b_v, L0_xattn_w_o, L0_xattn_b_o, L0_ffn_conf_w, L0_ffn_conf_b, L0_ffn_gate_w, L0_ffn_up_w, L0_ffn_down_w, L0_ffn_wealth):
    import jax
    import jax.numpy as jnp

    def _L0_xattn_ref(q, k, v, w_q, b_q, w_k, b_k, w_v, b_v, w_o, b_o):
        import jax, jax.numpy as jnp
        import numpy as np
        D_MODEL = 256
        N_HEADS = 16
        D_K = D_MODEL // N_HEADS
        B, S, _ = q.shape

        def proj(x, w, b):
            return (x @ w.T + b).reshape(B, S, N_HEADS, D_K).transpose(0, 2, 1, 3)
        qh = proj(q, w_q, b_q)
        kh = proj(k, w_k, b_k)
        vh = proj(v, w_v, b_v)
        scores = jnp.einsum('bhqd,bhkd->bhqk', qh, kh) / jnp.sqrt(jnp.asarray(D_K, jnp.float32))
        attn = jax.nn.softmax(scores, axis=-1)
        out = jnp.einsum('bhqk,bhkd->bhqd', attn, vh)
        out = out.transpose(0, 2, 1, 3).reshape(B, S, D_MODEL)
        return out @ w_o.T + b_o

    def _L0_ffn_ref(hidden_states, conf_w, conf_b, gate_w, up_w, down_w, wealth):
        import jax, jax.numpy as jnp
        import numpy as np
        E, K = (8, 2)
        x = hidden_states
        confidences = jax.nn.sigmoid(jnp.einsum('bsh,eh->bse', x, conf_w) + conf_b)
        bids = confidences * wealth
        top_bids, selected_experts = jax.lax.top_k(bids, K)
        sorted_bids = -jnp.sort(-bids, axis=-1)
        payments = jnp.broadcast_to(sorted_bids[..., K:K + 1], top_bids.shape)
        routing_weights = jax.nn.softmax(top_bids, axis=-1)
        combine = jnp.sum(jax.nn.one_hot(selected_experts, E, dtype=x.dtype) * routing_weights[..., None], axis=2)

        def ffn(gw, uw, dw):
            g = jnp.einsum('bsh,ih->bsi', x, gw)
            u = jnp.einsum('bsh,ih->bsi', x, uw)
            return jnp.einsum('bsi,hi->bsh', jax.nn.silu(g) * u, dw)
        expert_out = jax.vmap(ffn)(gate_w, up_w, down_w)
        output = jnp.einsum('ebsh,bse->bsh', expert_out, combine)
        return output
    x = x + jnp.tanh(g_xattn[0]) * _L0_xattn_ref(_layernorm(x, axis=-1), ctx_1024, ctx_1024, L0_xattn_w_q, L0_xattn_b_q, L0_xattn_w_k, L0_xattn_b_k, L0_xattn_w_v, L0_xattn_b_v, L0_xattn_w_o, L0_xattn_b_o)
    x = x + jnp.tanh(g_ffn[0]) * _L0_ffn_ref(_layernorm(x, axis=-1), L0_ffn_conf_w, L0_ffn_conf_b, L0_ffn_gate_w, L0_ffn_up_w, L0_ffn_down_w, L0_ffn_wealth)
    return x

_drawn_inputs = setup_inputs


def setup_inputs(seed=0):
    import zlib

    import numpy as np

    out = dict(_drawn_inputs(seed))
    spreads = {'L0_xattn_b_q': (0.0, 0.8),
     'L0_xattn_b_k': (0.0, 0.8),
     'L0_xattn_b_v': (0.0, 0.1),
     'L0_xattn_b_o': (0.0, 0.1),
     'L0_ffn_conf_b': (0.0, 0.1),
     'L0_ffn_wealth': (1.0, 0.2)}
    factors = {'L0_xattn_w_q': 7.883, 'L0_xattn_w_k': 8.0}
    for name, (base, spread) in spreads.items():
        noise = np.random.default_rng([zlib.crc32(name.encode()), seed]).standard_normal(out[name].shape)
        drawn = base * np.exp(spread * noise) if base else spread * noise
        out[name] = jnp.asarray(drawn.astype(out[name].dtype))
    for name, factor in factors.items():
        out[name] = (out[name] * factor).astype(out[name].dtype)
    return out
```

```python
import concourse.bass as bass
from concourse import mybir
from contextlib import ExitStack

BATCHES, SEQ, D = 16, 256, 256
HEADS, DK = 16, 16
EXPERTS, INNER = 8, 1024
P = 128
TOKENS = BATCHES * SEQ
HC = D // P
QT = SEQ // P
SLOT = 32
GROUPS = HEADS * SLOT // P
HPG = P // SLOT
TILE = 256
TT = TILE // P
REGION = TOKENS + TILE
ROW = 272
COMB = D
TOKCOL = D + EXPERTS
NCONST = 18
IC = INNER // P
PAIRS = IC // 2
WCOLS = 3 * HC * INNER
EPS = 1e-5
FAR = -3.0e38

fp32 = mybir.dt.float32
f32r = mybir.dt.float32r
i32 = mybir.dt.int32
ALU = mybir.AluOpType
ACT = mybir.ActivationFunctionType
AX = mybir.AxisListType


def build_program(nc, x, ctxT, wq, wk, wv, wo, bq, bk, bv, bo, confT, conf_b, wealth, g_attn, g_ffn,
                  gate_T, up_T, down_T, ident, tri, expert_row, expert_no, token_no, pad_rows, out):
    disp = nc.dram_tensor("dispatched", [EXPERTS * REGION, ROW], fp32, kind="Internal").ap()
    acc = nc.dram_tensor("accumulated", [TOKENS + TILE, D], fp32, kind="Internal").ap()

    with ExitStack() as keep:
        def sb(stack, name, shape, dt=fp32):
            return stack.enter_context(nc.sbuf_tensor(name, shape, dt))

        def sem(name):
            return keep.enter_context(nc.semaphore(name))

        stage = sb(keep, "stage", [P, WCOLS])
        hi0 = sb(keep, "w_hi0", [P, WCOLS], f32r)
        lo0 = sb(keep, "w_lo0", [P, WCOLS], f32r)
        idn = sb(keep, "idn", [P, P])
        counts = sb(keep, "counts", [P, EXPERTS], i32)
        tiles = sb(keep, "tiles", [P, EXPERTS], i32)

        s_stage = sem("stage_loaded")
        s_split = sem("weights_split")
        s_hi = sem("weights_hi")

        def load_stage(eng, e):
            third = WCOLS // 3
            if e:
                eng.wait_ge(s_split, 3 * e)
            eng.dma_start(stage[:, 0:third].rearrange("p (c n) -> p c n", c=HC),
                          gate_T[e].rearrange("(c p) n -> p c n", p=P)).then_inc(s_stage, 16)
            eng.dma_start(stage[:, third:2 * third].rearrange("p (c n) -> p c n", c=HC),
                          up_T[e].rearrange("(c p) n -> p c n", p=P)).then_inc(s_stage, 16)
            eng.dma_start(stage[:, 2 * third:].rearrange("p (c n) -> p c n", c=IC),
                          down_T[e].rearrange("(c p) n -> p c n", p=P)).then_inc(s_stage, 16)

        def split_weights(eng, e, hi, lo):
            third = WCOLS // 3
            eng.wait_ge(s_stage, 48 * (e + 1))
            for c in range(3):
                part = slice(c * third, (c + 1) * third)
                eng.tensor_copy(hi[:, part], stage[:, part]).then_inc(s_hi, 1)
                eng.wait_ge(s_hi, 3 * e + c + 1)
                eng.tensor_tensor(lo[:, part], stage[:, part], hi[:, part].bitcast(fp32),
                                  ALU.subtract).then_inc(s_split, 1)

        attention_stage(nc, sb, sem, load_stage, split_weights, disp, acc, x, ctxT, wq, wk, wv, wo,
                        bq, bk, bv, bo, confT, conf_b, wealth, g_attn, g_ffn, ident, tri,
                        expert_row, expert_no, token_no, pad_rows, idn, counts, tiles, hi0, lo0)
        expert_stage(nc, sb, sem, load_stage, split_weights, disp, acc, idn, tiles, hi0, lo0,
                     s_split, out)


class Alone:

    def __init__(self, eng, name, seen):
        self.eng, self.seen, self.register = eng, seen, eng.alloc_register(name)

    def wait_ge(self, semaphore, value):
        if not isinstance(value, int):
            self.eng.reg_mov(self.register, value)
            value = self.register
        self.eng.wait_ge(*self.seen)
        self.eng.wait_ge(semaphore, value)


def attention_stage(nc, sb_in, sem, load_stage, split_weights, disp, acc, x, ctxT, wq, wk, wv, wo,
                    bq, bk, bv, bo, confT, conf_b, wealth, g_attn, g_ffn, ident, tri,
                    expert_row, expert_no, token_no, pad_rows, idn, counts, tiles, hi0, lo0):
    with ExitStack() as own:
        def sb(name, shape, dt=fp32):
            return sb_in(own, name, shape, dt)

        x_all = sb("x_all", [P, BATCHES, QT, D])
        cT = [sb(f"ctxT{i}", [P, HC, SEQ]) for i in range(2)]
        wq_s = sb("wq_s", [P, HC, HEADS * SLOT])
        wk_s = sb("wk_s", [P, HC, HEADS * SLOT])
        wv_s = sb("wv_s", [P, HC, D])
        wo_s = sb("wo_s", [P, HC, D])
        bq_s = sb("bq_s", [P, GROUPS])
        bk_s = sb("bk_s", [P, GROUPS])
        bv_s = sb("bv_s", [P, D])
        bo_s = sb("bo_s", [P, D])
        conf_s = sb("conf_s", [P, HC, EXPERTS])
        cb_s = sb("cb_s", [P, QT, EXPERTS])
        wealth_s = sb("wealth_s", [P, QT, EXPERTS])
        eoff = sb("eoff", [P, QT, EXPERTS])
        eno = sb("eno", [P, QT, EXPERTS])
        tok = sb("tok", [P, BATCHES * QT], i32)
        tri_s = sb("tri_s", [P, P])
        ones = sb("ones", [P, P])
        pads = sb("pads", [P, TT, ROW])
        gates = sb("gates", [P, 2])
        tg = sb("tg", [P, 2])
        minus_half = sb("minus_half", [P, QT])
        stats = sb("stats", [P, QT, 6])
        mv = sb("mv", [P, QT, 2])
        rstd = sb("rstd", [P, QT])
        shift = sb("shift", [P, QT])
        stats2 = sb("stats2", [P, QT, 6])
        mv2 = sb("mv2", [P, QT, 2])
        rstd2 = sb("rstd2", [P, QT])
        shift2 = sb("shift2", [P, QT])
        xn = sb("xn", [P, QT, D])
        xT = sb("xT", [P, HC, SEQ])
        q = [sb(f"queries{i}", [P, GROUPS, SEQ]) for i in range(2)]
        k = [sb(f"keys{i}", [P, GROUPS, SEQ]) for i in range(2)]
        v = [sb(f"values{i}", [P, QT, HEADS, SLOT]) for i in range(2)]
        qr = sb("qr", [P, GROUPS, SEQ], f32r)
        kr = sb("kr", [P, GROUPS, SEQ], f32r)
        probs = [sb(f"probs{i}", [P, HPG, QT, SEQ]) for i in range(2)]
        mpad = sb("mpad", [P, QT, GROUPS, P])
        oS = sb("oS", [P, GROUPS, SEQ])
        rsum = sb("rsum", [P, QT, HEADS])
        on = sb("on", [P, QT, D])
        oT = sb("oT", [P, HC, SEQ])
        x2 = sb("x2", [P, QT, D])
        row = sb("row", [P, QT, ROW])
        x2T = sb("x2T", [P, HC, SEQ])
        z = sb("z", [P, QT, EXPERTS])
        ez = sb("ez", [P, QT, EXPERTS])
        bids = sb("bids", [P, QT, EXPERTS])
        t8 = sb("t8", [P, QT, EXPERTS])
        u8 = sb("u8", [P, QT, EXPERTS])
        bqs = sb("bqs", [P, GROUPS])
        m1 = sb("m1", [P, QT, EXPERTS])
        m2 = sb("m2", [P, QT, EXPERTS])
        m12 = sb("m12", [P, QT, EXPERTS])
        macc = sb("macc", [P, EXPERTS])
        v1 = sb("v1", [P, QT])
        v2 = sb("v2", [P, QT])
        r1 = sb("r1", [P, QT])
        dv = sb("dv", [P, QT])
        ed = sb("ed", [P, QT])
        w1 = sb("w1", [P, QT])
        c8 = sb("c8", [P, QT, EXPERTS])
        w2 = sb("w2", [P, QT])
        posf = sb("posf", [P, 2, QT])
        posi = sb("posi", [P, 2, QT], i32)

        scores = own.enter_context(nc.psum_tensor("scores", [P, HPG, QT, SEQ], fp32))
        maxps = own.enter_context(nc.psum_tensor("maxps", [P, 2, QT, SEQ], fp32))
        pv = own.enter_context(nc.psum_tensor("pv", [P, 512], fp32))
        misc = own.enter_context(nc.psum_tensor("misc", [P, 2, 256], fp32))


        names = """x_loaded ctx_loaded consts_loaded pads_loaded pads_stored consts_made constants_ready
            misc_written misc_read ln_stats ln_chain ln_scaled ln_done ln2_chain ln2_stats ln2_scaled
            ln2_done bias_added qr_copied kr_copied max_scored max_taken scored expd pv_done pv_read
            sums_inverted x2_stored sigmoid_half_ready route_chain masks_ready second_ready
            rows_chain rows_ready scattered counts_summed count_chain counted values_made
            scale_chain scale2_chain""".split()
        s = {n: sem(n) for n in names}

        FRONT = ["TX", "Q0", "K0", "Q1", "K1", "V", "MT0", "MT1"]
        FULL = ["TO0", "TX", "TO1", "TN", "Q0", "WO", "K0", "Q1", "TX2", "K1", "LG", "V", "RK", "MT0", "MT1"]
        BACK = ["TO0", "TO1", "TN", "WO", "TX2", "LG", "RK"]

        class Use:

            def __init__(self, order, before):
                self.order, self.before = order, before

            def free(self, eng, what):
                n = self.before + self.order.index(what)
                if not (isinstance(n, int) and n == 0):
                    eng.wait_ge(s["misc_read"], n)

            def after(self, what):
                return self.before + (self.order.index(what) + 1)

            def written(self, eng, what):
                eng.wait_ge(s["misc_written"], self.after(what))

            def read(self, eng, what):
                eng.wait_ge(s["misc_read"], self.after(what))

        def full_use(b):
            return Use(FULL, b * len(FULL) + (2 * len(FRONT) - len(FULL)))

        PROLOGUE = Use(FRONT, 0)
        ITERATION0 = Use(FRONT, len(FRONT))
        before_last = (BATCHES - 1) * len(FULL) + 2 * len(FRONT) - len(FULL)
        LAST = Use(BACK, before_last)
        EPILOGUE = Use(BACK, before_last + len(BACK))

        def over_batches(eng, body):
            body(0, 0, ITERATION0, True, False)
            with eng.Fori(0, BATCHES // 2 - 1) as i:
                for b, par in ((i * 2 + 1, 1), (i * 2 + 2, 0)):
                    body(b, par, full_use(b), True, True)
            body(BATCHES - 1, 1, LAST, False, True)

        def is_first(b):
            return isinstance(b, int) and b == 0

        def chain(eng, name, each, b):
            n = [0]

            def link(instruction):
                n[0] += 1
                assert n[0] <= each
                instruction.then_inc(s[name], 1)
                eng.wait_ge(s[name], b * each + n[0])
            return link

        block = own.enter_context(nc.Block())

        @block.sync
        def _(sp):
            def load_x(b):
                sp.dma_start(x_all[:, b], x[b].rearrange("(t p) d -> p t d", p=P)).then_inc(s["x_loaded"], 16)

            load_x(0)
            sp.dma_start(cT[0][:], ctxT[0].rearrange("(c p) s -> p c s", p=P)).then_inc(s["ctx_loaded"], 16)
            consts = ((idn[:], ident), (wq_s[:], wq.rearrange("(c p) n -> p c n", p=P)), (bq_s[:], bq),
                      (wk_s[:], wk.rearrange("(c p) n -> p c n", p=P)), (bk_s[:], bk),
                      (wv_s[:], wv.rearrange("(c p) n -> p c n", p=P)), (bv_s[:], bv),
                      (gates[:, 0:1], g_attn), (gates[:, 1:2], g_ffn), (bo_s[:], bo),
                      (wo_s[:], wo.rearrange("(c p) n -> p c n", p=P)),
                      (conf_s[:], confT.rearrange("(c p) n -> p c n", p=P)), (cb_s[:], conf_b),
                      (wealth_s[:], wealth), (eoff[:], expert_row), (eno[:], expert_no),
                      (tri_s[:], tri), (tok[:], token_no))
            assert len(consts) == NCONST
            for to, of in consts:
                sp.dma_start(to, of).then_inc(s["consts_loaded"], 16)
            sp.dma_start(pads[:], pad_rows.rearrange("(t p) d -> p t d", p=P)).then_inc(s["pads_loaded"], 16)
            sp.wait_ge(s["ctx_loaded"], 16)
            sp.dma_start(cT[1][:], ctxT[1].rearrange("(c p) s -> p c s", p=P)).then_inc(s["ctx_loaded"], 16)
            for b in range(1, BATCHES):
                sp.wait_ge(s["x_loaded"], 16 * b)
                load_x(b)
            sp.wait_ge(s["pads_loaded"], 16)
            sp.dma_start(acc[TOKENS:].rearrange("(t p) d -> p t d", p=P), pads[:, :, 0:D]).then_inc(s["pads_stored"], 16)

            def store_residual(b, use):
                use.read(sp, "WO")
                sp.dma_start(acc[bass.ds(b * SEQ, SEQ)].rearrange("(t p) d -> p t d", p=P), x2[:]).then_inc(s["x2_stored"], 16)

            def body(b, par, use, front, back):
                if back:
                    store_residual(b - 1, use)
                    if front:
                        sp.dma_start(cT[1 - par][:], ctxT[bass.ds(b + 1, 1)].rearrange("o (c p) s -> p (o c) s", p=P)).then_inc(s["ctx_loaded"], 16)

            over_batches(sp, body)
            store_residual(BATCHES - 1, EPILOGUE)
            sp.wait_ge(s["counted"], 1)
            for e in range(EXPERTS):
                n = sp.value_load(counts[0:1, e:e + 1], min_val=0, max_val=TOKENS)
                sp.dma_start(disp[bass.ds(n + e * REGION, TILE)].rearrange("(t p) d -> p t d", p=P),
                             pads[:]).then_inc(s["pads_stored"], 16)
            sp.wait_ge(s["x2_stored"], 16 * BATCHES)
            sp.wait_ge(s["pads_stored"], 16 + 16 * EXPERTS)

        @block.tensor
        def _(pe):
            mm = nc.tensor.matmul

            def turn(source, what, use):
                use.free(pe, what)
                for t in range(QT):
                    for c in range(HC):
                        last = nc.tensor.transpose(misc[:, c, t * P:(t + 1) * P], source[:, t, c * P:(c + 1) * P], idn[:])
                last.then_inc(s["misc_written"], 1)

            def turn_x(b, use):
                pe.wait_ge(s["ln_done"], b * QT + QT)
                turn(xn, "TX", use)

            def project(weights, source, what, half_, use):
                use.free(pe, f"{what}{half_}")
                for g in range(2):
                    for c in range(HC):
                        cols = (2 * half_ + g) * P
                        last = mm(misc[:, g, :], weights[:, c, cols:cols + P], source[:, c, :], start=c == 0, stop=c == HC - 1)
                last.then_inc(s["misc_written"], 1)

            def project_q(half_, use):
                if half_ == 0:
                    use.read(pe, "TX")
                project(wq_s, xT, "Q", half_, use)

            def project_k(b, par, half_, use):
                if half_ == 0:
                    pe.wait_ge(s["ctx_loaded"], b * 16 + 16)
                project(wk_s, cT[par], "K", half_, use)

            def project_v(par, use):
                use.free(pe, "V")
                for t in range(QT):
                    for c in range(HC):
                        last = mm(misc[:, t, :], cT[par][:, c, t * P:(t + 1) * P], wv_s[:, c, :], start=c == 0, stop=c == HC - 1)
                last.then_inc(s["misc_written"], 1)

            def max_scores(b, pair):
                g, j0 = pair // 2, 2 * (pair % 2)
                if pair % 4 == 0:
                    pe.wait_ge(s["qr_copied"], b * 2 + (pair // 4 + 1))
                    pe.wait_ge(s["kr_copied"], b * 2 + (pair // 4 + 1))
                if not (is_first(b) and pair == 0):
                    pe.wait_ge(s["max_taken"], b * (2 * GROUPS) + pair)
                for t in range(QT):
                    for j in range(2):
                        r = slice((j0 + j) * SLOT, (j0 + j + 1) * SLOT)
                        last = mm(maxps[:, j, t, :], qr[r, g, t * P:(t + 1) * P], kr[r, g, :], start=True, stop=True)
                last.then_inc(s["max_scored"], 1)

            def max_rows(b, half_, use):
                pe.wait_ge(s["max_taken"], b * (2 * GROUPS) + 4 * (half_ + 1))
                use.free(pe, f"MT{half_}")
                for g in range(2):
                    for t in range(QT):
                        last = mm(misc[:, g, t * P:(t + 1) * P], mpad[:, t, 2 * half_ + g, :], idn[:], start=True, stop=True)
                last.then_inc(s["misc_written"], 1)

            def score(b, par, g):
                if g % 2 == 0:
                    pe.wait_ge(s["misc_read"], (len(FRONT) - 1 if is_first(b) else b * len(FULL)) + g // 2)
                if not (is_first(b) and g == 0):
                    pe.wait_ge(s["expd"], b * (2 * GROUPS) + 2 * g)
                for t in range(QT):
                    for j in range(HPG):
                        r = slice(j * SLOT, (j + 1) * SLOT)
                        last = mm(scores[:, j, t, :], k[par][r, g, t * P:(t + 1) * P], q[par][r, g, :], start=True, stop=True)
                last.then_inc(s["scored"], 1)

            def weigh(b, par, g):
                pe.wait_ge(s["expd"], b * (2 * GROUPS) + 2 * (g + 1))
                if not (is_first(b) and g == 0):
                    pe.wait_ge(s["pv_read"], b * GROUPS + g)
                for t in range(QT):
                    for j in range(HPG):
                        last = mm(pv[j * SLOT:(j + 1) * SLOT, 0:SEQ], v[par][:, t, g * HPG + j, :], probs[g % 2][:, j, t, :],
                                  start=t == 0, stop=t == QT - 1)
                last.then_inc(s["pv_done"], 1)

            def turn_heads(b, t, use):
                if t == 0:
                    pe.wait_ge(s["pv_read"], b * GROUPS + GROUPS)
                use.free(pe, f"TO{t}")
                for g in range(GROUPS):
                    last = nc.tensor.transpose(misc[:, g // 2, (g % 2) * P:(g % 2 + 1) * P], oS[:, g, t * P:(t + 1) * P], idn[:])
                last.then_inc(s["misc_written"], 1)

            def turn_normed(use):
                use.read(pe, "TO1")
                turn(on, "TN", use)

            def attn_out(use):
                use.read(pe, "TN")
                use.free(pe, "WO")
                for t in range(QT):
                    for c in range(HC):
                        last = mm(misc[:, t, :], oT[:, c, t * P:(t + 1) * P], wo_s[:, c, :], start=c == 0, stop=c == HC - 1)
                last.then_inc(s["misc_written"], 1)

            def turn_x2(b, use):
                pe.wait_ge(s["ln2_done"], b * QT + QT)
                turn(row, "TX2", use)

            def logits(use):
                use.read(pe, "TX2")
                use.free(pe, "LG")
                for t in range(QT):
                    for c in range(HC):
                        last = mm(misc[:, t, 0:EXPERTS], x2T[:, c, t * P:(t + 1) * P], conf_s[:, c, :], start=c == 0, stop=c == HC - 1)
                last.then_inc(s["misc_written"], 1)

            def ranks(b, use):
                pe.wait_ge(s["masks_ready"], b + 1)
                use.free(pe, "RK")
                for t in range(QT):
                    mm(misc[:, t, 0:EXPERTS], tri_s[:], m12[:, t, :], start=True, stop=False)
                    if t == 1:
                        mm(misc[:, t, 0:EXPERTS], ones[:], m12[:, 0, :], start=False, stop=False)
                    last = mm(misc[:, t, 0:EXPERTS], ones[:], macc[:], start=False, stop=True)
                last.then_inc(s["misc_written"], 1)

            pe.wait_ge(s["consts_loaded"], 16 * NCONST)
            pe.wait_ge(s["constants_ready"], 1)
            turn_x(0, PROLOGUE)
            project_q(0, PROLOGUE)
            project_k(0, 0, 0, PROLOGUE)
            project_q(1, PROLOGUE)
            project_k(0, 0, 1, PROLOGUE)
            project_v(0, PROLOGUE)
            for half_ in range(2):
                for pair in range(4 * half_, 4 * half_ + 4):
                    max_scores(0, pair)
                max_rows(0, half_, PROLOGUE)

            def body(b, par, use, front, back):
                nxt = 1 - par
                score(b, par, 0)
                if back:
                    turn_heads(b - 1, 0, use)
                if front:
                    turn_x(b + 1, use)
                if back:
                    turn_heads(b - 1, 1, use)
                score(b, par, 1)
                if back:
                    turn_normed(use)
                if front:
                    project_q(0, use)
                weigh(b, par, 0)
                if back:
                    attn_out(use)
                if front:
                    project_k(b + 1, nxt, 0, use)
                score(b, par, 2)
                if front:
                    max_scores(b + 1, 0)
                    project_q(1, use)
                    max_scores(b + 1, 1)
                weigh(b, par, 1)
                if back:
                    turn_x2(b - 1, use)
                if front:
                    project_k(b + 1, nxt, 1, use)
                    max_scores(b + 1, 2)
                score(b, par, 3)
                if front:
                    max_scores(b + 1, 3)
                if back:
                    logits(use)
                if front:
                    project_v(nxt, use)
                weigh(b, par, 2)
                if front:
                    max_scores(b + 1, 4)
                    max_scores(b + 1, 5)
                if back:
                    ranks(b - 1, use)
                if front:
                    max_scores(b + 1, 6)
                    max_rows(b + 1, 0, use)
                weigh(b, par, 3)
                if front:
                    max_scores(b + 1, 7)
                    max_rows(b + 1, 1, use)

            over_batches(pe, body)
            last_batch = BATCHES - 1
            turn_heads(last_batch, 0, EPILOGUE)
            turn_heads(last_batch, 1, EPILOGUE)
            turn_normed(EPILOGUE)
            attn_out(EPILOGUE)
            turn_x2(last_batch, EPILOGUE)
            logits(EPILOGUE)
            ranks(last_batch, EPILOGUE)
            pe.wait_ge(s["counts_summed"], 2 * BATCHES)
            mm(misc[:, 0, 0:EXPERTS], ones[:], macc[:], start=True, stop=True).then_inc(s["misc_written"], 1)

        @block.scalar
        def _(act):
            def exps(b, g):
                act.wait_ge(s["scored"], b * GROUPS + (g + 1))
                if not (is_first(b) and g < 2):
                    act.wait_ge(s["pv_done"], b * GROUPS + (g - 1))
                for h in range(2):
                    nc.scalar.activation(probs[g % 2][:, 2 * h:2 * h + 2], scores[:, 2 * h:2 * h + 2], ACT.Exp).then_inc(s["expd"], 1)

            def norm_x(b):
                act.wait_ge(s["ln_scaled"], b + 1)
                for t in range(QT):
                    nc.scalar.activation(xn[:, t, :], x_all[:, bass.ds(b, 1), t, :].rearrange("p o d -> p (o d)"), ACT.Identity,
                                         bias=shift[:, t:t + 1], scale=rstd[:, t:t + 1]).then_inc(s["ln_done"], 1)

            def norm_x2(b):
                act.wait_ge(s["ln2_scaled"], b + 1)
                if not is_first(b):
                    act.wait_ge(s["scattered"], b * (16 * 2 * QT))
                for t in range(QT):
                    nc.scalar.activation(row[:, t, 0:D], x2[:, t, :], ACT.Identity, bias=shift2[:, t:t + 1],
                                         scale=rstd2[:, t:t + 1]).then_inc(s["ln2_done"], 1)

            def read_whole(to, what, use):
                use.written(act, what)
                nc.scalar.activation(to, misc[:], ACT.Copy).then_inc(s["misc_read"], 1)

            def read_q(par, half_, use):
                use.written(act, f"Q{half_}")
                for n in range(2 * half_, 2 * half_ + 2):
                    last = nc.scalar.activation(q[par][:, n, :], misc[:, n % 2, :], ACT.Identity, bias=bqs[:, n:n + 1], scale=DK ** -0.5)
                last.then_inc(s["misc_read"], 1)

            def read_k(par, half_, use):
                use.written(act, f"K{half_}")
                for n in range(2 * half_, 2 * half_ + 2):
                    last = nc.scalar.activation(k[par][:, n, :], misc[:, n % 2, :], ACT.Identity, bias=bk_s[:, n:n + 1], scale=1.0)
                last.then_inc(s["misc_read"], 1)

            def read_pv(b, g):
                act.wait_ge(s["pv_done"], b * GROUPS + (g + 1))
                nc.scalar.activation(oS[:, g, :], pv[:, 0:SEQ], ACT.Copy).then_inc(s["pv_read"], 1)

            def sigmoid(use):
                use.read(act, "LG")
                nc.scalar.activation(ez[:], z[:], ACT.Exp, scale=-1.0).then_inc(s["sigmoid_half_ready"], 1)

            def second_weight(b):
                act.wait_ge(s["masks_ready"], b + 1)
                nc.scalar.activation(ed[:], dv[:], ACT.Exp).then_inc(s["second_ready"], 1)

            act.wait_ge(s["consts_loaded"], 16 * NCONST)
            nc.scalar.activation(tg[:], gates[:], ACT.Tanh).then_inc(s["consts_made"], 1)
            nc.scalar.activation(bqs[:], bq_s[:], ACT.Copy, scale=DK ** -0.5).then_inc(s["consts_made"], 1)
            act.wait_ge(s["consts_made"], 2)
            norm_x(0)
            read_whole(xT[:], "TX", PROLOGUE)
            for half_ in range(2):
                read_q(0, half_, PROLOGUE)
                read_k(0, half_, PROLOGUE)

            def body(b, par, use, front, back):
                nxt = 1 - par
                exps(b, 0)
                if front:
                    norm_x(b + 1)
                    read_whole(xT[:], "TX", use)
                exps(b, 1)
                if back:
                    read_whole(oT[:], "TN", use)
                if front:
                    read_q(nxt, 0, use)
                read_pv(b, 0)
                if front:
                    read_k(nxt, 0, use)
                exps(b, 2)
                if front:
                    read_q(nxt, 1, use)
                read_pv(b, 1)
                if back:
                    norm_x2(b - 1)
                    read_whole(x2T[:], "TX2", use)
                if front:
                    read_k(nxt, 1, use)
                exps(b, 3)
                if back:
                    sigmoid(use)
                read_pv(b, 2)
                if back:
                    second_weight(b - 1)
                read_pv(b, 3)

            over_batches(act, body)
            read_whole(oT[:], "TN", EPILOGUE)
            norm_x2(BATCHES - 1)
            read_whole(x2T[:], "TX2", EPILOGUE)
            sigmoid(EPILOGUE)
            second_weight(BATCHES - 1)

        @block.vector
        def _(dve):
            V = nc.vector
            alone = Alone(dve, "dve_awaited", (s["consts_made"], 2))
            both8 = [P, QT, EXPERTS]

            def spread(column):
                return column[:].unsqueeze(2).to_broadcast(both8)

            def stats_x(b):
                dve.wait_ge(s["x_loaded"], b * 16 + 16)
                link = chain(alone, "ln_chain", QT, b)
                for t in range(QT):
                    link(V.bn_stats(stats[:, t, :], x_all[:, bass.ds(b, 1), t, :].rearrange("p o d -> p (o d)")))
                if not is_first(b):
                    alone.wait_ge(s["ln_done"], b * QT)
                for t in range(QT):
                    last = V.bn_aggr(mv[:, t, :], stats[:, t, :])
                last.then_inc(s["ln_stats"], 1)

            def norm_heads(b, t, use):
                use.written(dve, f"TO{t}")
                heads = misc[:].rearrange("p a (h c) -> p (a h) c", c=SLOT)
                V.reciprocal(rsum[:, t, :], heads[:, :, DK]).then_inc(s["sums_inverted"], 1)
                dve.wait_ge(s["sums_inverted"], b * QT + (t + 1))
                V.tensor_tensor(on[:, t, :].rearrange("p (h d) -> p h d", d=DK), heads[:, :, 0:DK],
                                rsum[:, t, :].unsqueeze(2).to_broadcast([P, HEADS, DK]), ALU.mult).then_inc(s["misc_read"], 1)

            def residual(b, use):
                use.written(dve, "WO")
                dve.wait_ge(s["bias_added"], b + 1)
                if not is_first(b):
                    dve.wait_ge(s["x2_stored"], b * 16)
                    dve.wait_ge(s["ln2_done"], b * QT)
                V.scalar_tensor_tensor(x2[:].rearrange("p t d -> p (t d)"), misc[:].rearrange("p t d -> p (t d)"), tg[:, 0:1],
                                       x_all[:, bass.ds(b, 1)].rearrange("p o t d -> p (o t d)"), ALU.mult, ALU.add).then_inc(s["misc_read"], 1)
                use.read(dve, "WO")
                link = chain(alone, "ln2_chain", QT, b)
                for t in range(QT):
                    link(V.bn_stats(stats2[:, t, :], x2[:, t, :]))
                for t in range(QT):
                    last = V.bn_aggr(mv2[:, t, :], stats2[:, t, :])
                last.then_inc(s["ln2_stats"], 1)

            def read_v(par, use):
                use.written(dve, "V")
                for t in range(QT):
                    last = V.tensor_tensor(v[par][:, t, :, 0:DK], misc[:, t, :].rearrange("p (h d) -> p h d", d=DK),
                                           bv_s[:].rearrange("p (h d) -> p h d", d=DK), ALU.add)
                last.then_inc(s["misc_read"], 1)

            def maxima(b, pair):
                g, j0 = pair // 2, 2 * (pair % 2)
                dve.wait_ge(s["max_scored"], b * (2 * GROUPS) + (pair + 1))
                to = mpad[:, :, g, j0 * SLOT:(j0 + 2) * SLOT].rearrange("p t (j c) -> p j t c", c=SLOT)[:, :, :, DK]
                V.tensor_reduce(to, maxps[:], AX.X, ALU.max, negate=True).then_inc(s["max_taken"], 1)

            def shift_q(par, half_, use):
                use.written(dve, f"MT{half_}")
                V.tensor_tensor(q[par][:, 2 * half_:2 * half_ + 2, :], q[par][:, 2 * half_:2 * half_ + 2, :], misc[:], ALU.add).then_inc(s["misc_read"], 1)

            def read_logits(b, use):
                use.written(dve, "LG")
                V.tensor_tensor(z[:], misc[:, :, 0:EXPERTS], cb_s[:], ALU.add).then_inc(s["misc_read"], 1)

            def top_two(b):
                dve.wait_ge(s["sigmoid_half_ready"], b + 1)
                link = chain(dve, "route_chain", 14, b)
                link(V.tensor_scalar(t8[:], ez[:], 1.0, None, ALU.add))
                link(V.reciprocal(u8[:], t8[:]))
                link(V.tensor_tensor(bids[:], u8[:], wealth_s[:], ALU.mult))
                link(V.tensor_reduce(v1[:], bids[:], AX.X, ALU.max))
                link(V.tensor_tensor(t8[:], bids[:], spread(v1), ALU.is_equal))
                link(V.scalar_tensor_tensor(u8[:], t8[:], -float(EXPERTS), eno[:], ALU.mult, ALU.add))
                link(V.tensor_reduce(r1[:], u8[:], AX.X, ALU.min))
                link(V.tensor_tensor(m1[:], u8[:], spread(r1), ALU.is_equal))
                link(V.scalar_tensor_tensor(bids[:], m1[:], FAR, bids[:], ALU.mult, ALU.add))
                link(V.tensor_reduce(v2[:], bids[:], AX.X, ALU.max))
                V.tensor_tensor(dv[:], v2[:], v1[:], ALU.subtract)
                link(V.tensor_tensor(t8[:], bids[:], spread(v2), ALU.is_equal))
                link(V.scalar_tensor_tensor(u8[:], t8[:], -float(EXPERTS), eno[:], ALU.mult, ALU.add))
                link(V.tensor_reduce(r1[:], u8[:], AX.X, ALU.min))
                link(V.tensor_tensor(m2[:], u8[:], spread(r1), ALU.is_equal))
                V.tensor_tensor(m12[:], m1[:], m2[:], ALU.add).then_inc(s["masks_ready"], 1)

            def positions(b, use):
                use.written(dve, "RK")
                V.tensor_tensor(u8[:], misc[:, :, 0:EXPERTS], eoff[:], ALU.add).then_inc(s["misc_read"], 1)
                for t in range(QT):
                    V.tensor_tensor(macc[:], macc[:], m12[:, t, :], ALU.add).then_inc(s["counts_summed"], 1)
                    dve.wait_ge(s["counts_summed"], b * QT + (t + 1))
                link = chain(dve, "rows_chain", 11, b)
                link(V.tensor_tensor(t8[:], m1[:], u8[:], ALU.mult))
                link(V.tensor_reduce(posf[:, 0, :], t8[:], AX.X, ALU.add))
                link(V.tensor_tensor(t8[:], m2[:], u8[:], ALU.mult))
                link(V.tensor_reduce(posf[:, 1, :], t8[:], AX.X, ALU.add))
                V.tensor_copy(posi[:], posf[:])
                dve.wait_ge(s["second_ready"], b + 1)
                link(V.tensor_scalar(w2[:], ed[:], 1.0, None, ALU.add))
                link(V.reciprocal(w1[:], w2[:]))
                link(V.tensor_scalar(w1[:], w1[:], tg[:, 1:2], None, ALU.mult))
                link(V.tensor_tensor(w2[:], w1[:], ed[:], ALU.mult))
                link(V.tensor_tensor(t8[:], m1[:], spread(w1), ALU.mult))
                link(V.tensor_tensor(c8[:], m2[:], spread(w2), ALU.mult))
                link(V.tensor_copy(row[:, :, TOKCOL:TOKCOL + 1].bitcast(i32),
                                   tok[:, bass.ds(b * QT, QT)].unsqueeze(2)))
                V.tensor_tensor(row[:, :, COMB:COMB + EXPERTS], t8[:], c8[:], ALU.add).then_inc(s["rows_ready"], 1)

            V.memset(v[0][:], 1.0)
            V.memset(v[1][:], 1.0)
            V.memset(mpad[:], 0.0)
            V.memset(macc[:], 0.0)
            V.memset(row[:, :, D:], 0.0)
            V.memset(minus_half[:], -0.5)
            V.memset(ones[:], 1.0).then_inc(s["constants_ready"], 1)
            dve.wait_ge(s["constants_ready"], 1)
            dve.wait_ge(s["consts_loaded"], 16 * NCONST)
            dve.wait_ge(s["consts_made"], 2)
            stats_x(0)
            read_v(0, PROLOGUE)
            for half_ in range(2):
                for pair in range(4 * half_, 4 * half_ + 4):
                    maxima(0, pair)
                shift_q(0, half_, PROLOGUE)

            def body(b, par, use, front, back):
                nxt = 1 - par
                if front:
                    stats_x(b + 1)
                if back:
                    norm_heads(b - 1, 0, use)
                    norm_heads(b - 1, 1, use)
                    residual(b - 1, use)
                if front:
                    for pair in range(4):
                        maxima(b + 1, pair)
                if back:
                    read_logits(b - 1, use)
                if front:
                    read_v(nxt, use)
                if back:
                    top_two(b - 1)
                if front:
                    maxima(b + 1, 4)
                    maxima(b + 1, 5)
                if back:
                    positions(b - 1, use)
                if front:
                    maxima(b + 1, 6)
                    shift_q(nxt, 0, use)
                    maxima(b + 1, 7)
                    shift_q(nxt, 1, use)

            over_batches(dve, body)
            b = BATCHES - 1
            norm_heads(b, 0, EPILOGUE)
            norm_heads(b, 1, EPILOGUE)
            residual(b, EPILOGUE)
            read_logits(b, EPILOGUE)
            top_two(b)
            positions(b, EPILOGUE)
            dve.wait_ge(s["misc_written"], EPILOGUE.before + len(BACK) + 1)
            link = chain(dve, "count_chain", 4, 0)
            link(V.tensor_copy(counts[:], misc[:, 0, 0:EXPERTS]))
            link(V.tensor_scalar(tiles[:], misc[:, 0, 0:EXPERTS], float(TILE - 1), None, ALU.add))
            link(V.tensor_single_scalar(tiles[:], tiles[:], TILE.bit_length() - 1, ALU.arith_shift_right))
            V.tensor_scalar(tiles[:], tiles[:], 1, None, ALU.max).then_inc(s["counted"], 1)
            dve.wait_ge(s["counted"], 1)

        @block.gpsimd
        def _(pool):
            G = nc.gpsimd
            alone = Alone(pool, "pool_awaited", (s["consts_made"], 2))

            def scale_of(b, name, stats_ready, mv_, rstd_, shift_, done):
                alone.wait_ge(s[stats_ready], b + 1)
                link = chain(alone, name, 3, b)
                link(G.tensor_scalar(rstd_[:], mv_[:, :, 1], EPS, None, ALU.add))
                link(G.tensor_tensor(rstd_[:], rstd_[:], minus_half[:], ALU.pow))
                link(G.tensor_tensor(shift_[:], mv_[:, :, 0], rstd_[:], ALU.mult))
                G.tensor_scalar(shift_[:], shift_[:], -1.0, None, ALU.mult).then_inc(s[done], 1)

            def scale_x(b):
                scale_of(b, "scale_chain", "ln_stats", mv, rstd, shift, "ln_scaled")

            def add_bias(b):
                pool.wait_ge(s["ln_done"], b * QT + QT)
                xb = x_all[:, bass.ds(b, 1)].rearrange("p o t d -> p (o t) d")
                G.tensor_tensor(xb, xb, bo_s[:].unsqueeze(1).to_broadcast([P, QT, D]), ALU.add).then_inc(s["bias_added"], 1)

            def round_half(to, of, what, name, par, half_, use):
                alone.wait_ge(s["misc_read"], use.after(f"{what}{half_}"))
                G.tensor_copy(to[:, 2 * half_:2 * half_ + 2, :], of[par][:, 2 * half_:2 * half_ + 2, :]).then_inc(s[name], 1)

            def round_q(par, half_, use):
                round_half(qr, q, "Q", "qr_copied", par, half_, use)

            def round_k(par, half_, use):
                round_half(kr, k, "K", "kr_copied", par, half_, use)

            def scatter(b):
                alone.wait_ge(s["rows_ready"], b + 1)
                for t in range(QT):
                    for c in range(2):
                        pool.indirect_dma_start(disp, bass.IndirectOffsetOnAxis(posi[:, c, t:t + 1], axis=0),
                                                row[:, t, :], None).then_inc(s["scattered"], 16)

            load_stage(pool, 0)
            pool.wait_ge(s["constants_ready"], 1)
            pool.wait_ge(s["consts_loaded"], 16 * NCONST)
            pool.wait_ge(s["consts_made"], 2)
            scale_x(0)
            G.tensor_scalar(bo_s[:], bo_s[:], tg[:, 0:1], None, ALU.mult).then_inc(s["values_made"], 1)
            pool.wait_ge(s["values_made"], 1)
            add_bias(0)
            for half_ in range(2):
                round_q(0, half_, PROLOGUE)
                round_k(0, half_, PROLOGUE)

            def body(b, par, use, front, back):
                nxt = 1 - par
                if front:
                    scale_x(b + 1)
                if back:
                    scale_of(b - 1, "scale2_chain", "ln2_stats", mv2, rstd2, shift2, "ln2_scaled")
                if front:
                    for half_ in range(2):
                        round_q(nxt, half_, use)
                        round_k(nxt, half_, use)
                    add_bias(b + 1)
                if back:
                    scatter(b - 1)
                if not back:
                    split_weights(pool, 0, hi0, lo0)
                    load_stage(pool, 1)

            over_batches(pool, body)
            scale_of(BATCHES - 1, "scale2_chain", "ln2_stats", mv2, rstd2, shift2, "ln2_scaled")
            scatter(BATCHES - 1)
            pool.wait_ge(s["scattered"], BATCHES * 16 * 2 * QT)


def expert_stage(nc, sb_in, sem, load_stage, split_weights, disp, acc, idn, tiles, hi0, lo0, s_split, out):
    with ExitStack() as own:
        def sb(name, shape, dt=fp32):
            return sb_in(own, name, shape, dt)

        hi = [hi0, sb("w_hi1", [P, WCOLS], f32r)]
        lo = [lo0, sb("w_lo1", [P, WCOLS], f32r)]
        xg = sb("xg", [P, TT, ROW])
        x_hi = sb("x_hi", [P, HC, TILE], f32r)
        x_lo = sb("x_lo", [P, HC, TILE], f32r)
        silu = [sb(f"silu{i}", [P, 2, TILE]) for i in range(2)]
        h = [sb(f"h{i}", [P, 2, TILE]) for i in range(2)]
        h_hi = sb("h_hi", [P, IC, TILE], f32r)
        h_lo = sb("h_lo", [P, IC, TILE], f32r)
        weight = sb("weight", [P, TT])
        token = sb("token", [P, TT], i32)
        y = sb("y", [P, TT, D])
        note = sb("note", [P, 4])

        turned = own.enter_context(nc.psum_tensor("turned", [P, HC, TILE], fp32))
        gate = [own.enter_context(nc.psum_tensor(f"gate{i}", [P, 2, TILE], fp32)) for i in range(2)]
        up = [own.enter_context(nc.psum_tensor(f"up{i}", [P, 2, TILE], fp32)) for i in range(2)]
        down = [own.enter_context(nc.psum_tensor(f"down{i}", [P, 512], fp32)) for i in range(TT)]

        s_rows = sem("rows_loaded")
        s_turned = sem("rows_turned")
        s_xhi = sem("x_hi_ready")
        s_xlo = sem("x_lo_ready")
        s_noted = sem("weights_and_tokens_noted")
        s_pair = sem("gate_up_written")
        s_silu = sem("silu_done")
        s_made = sem("gate_up_empty")
        s_hhi = sem("h_hi_ready")
        s_hlo = sem("h_lo_ready")
        s_down = sem("down_written")
        s_y = sem("down_read")
        s_added = sem("added")
        s_all = sem("all_added")
        s_out = sem("out_stored")

        def weights(par, which, mat):
            third = WCOLS // 3
            return which[par][:, mat * third:(mat + 1) * third].rearrange("p (c n) -> p c n", c=IC if mat == 2 else HC)

        def over_tiles(eng, name, before_expert, tile):
            n = eng.alloc_register(name)
            eng.reg_mov(n, 0)
            for e in range(EXPERTS):
                before_expert(e, eng.snap(n))
                trips = eng.value_load(tiles[0:1, e:e + 1], min_val=1, max_val=TOKENS // TILE)
                with eng.Fori(0, trips) as j:
                    tile(e, j, eng.snap(n))
                    eng.reg_add(n, n, 1)
            return eng.snap(n)

        block = own.enter_context(nc.Block())

        @block.sync
        def _(sp):
            def load_rows(first_row):
                sp.dma_start(xg[:], disp[bass.ds(first_row, TILE)].rearrange("(t p) d -> p t d", p=P)).then_inc(s_rows, 16)

            def tile(e, j, n):
                sp.wait_ge(s_noted, n)
                load_rows(j * TILE + e * REGION)

            total = over_tiles(sp, "sp_count", lambda e, n: None, tile)
            sp.wait_ge(s_noted, total)
            load_rows(0)
            sp.wait_ge(s_all, 1)
            half = TOKENS // 2
            flat = out.rearrange("b s d -> (b s) d")
            sp.dma_start(flat[0:half], acc[0:half]).then_inc(s_out, 16)
            sp.wait_ge(s_out, 32)

        @block.tensor
        def _(pe):
            mm = nc.tensor.matmul

            def turn_rows(after_load):
                pe.wait_ge(s_rows, after_load)
                for t in range(TT):
                    for c in range(HC):
                        last = nc.tensor.transpose(turned[:, c, t * P:(t + 1) * P], xg[:, t, c * P:(c + 1) * P], idn[:])
                last.then_inc(s_turned, 1)

            def gate_up(par, pair, n):
                pe.wait_ge(s_made, n * PAIRS + (pair + 1))
                for mat, bank in ((0, gate[pair % 2]), (1, up[pair % 2])):
                    for i in range(2):
                        cols = slice((2 * pair + i) * P, (2 * pair + i + 1) * P)
                        terms = [(w, r, c) for w, r in ((hi, x_hi), (hi, x_lo), (lo, x_hi)) for c in range(HC)]
                        for m, (w, r, c) in enumerate(terms):
                            last = mm(bank[:, i, :], weights(par, w, mat)[:, c, cols], r[:, c, :],
                                      start=m == 0, stop=m == len(terms) - 1)
                last.then_inc(s_pair, 1)

            def contract(par, pair, n):
                pe.wait_ge(s_hlo, n * PAIRS + (pair + 1))
                if pair == 0:
                    pe.wait_ge(s_y, n * TT)
                for i in (2 * pair, 2 * pair + 1):
                    for t in range(TT):
                        for m, (r, w) in enumerate(((h_hi, hi), (h_lo, hi), (h_hi, lo))):
                            last = mm(down[t][:, 0:D], r[:, i, t * P:(t + 1) * P], weights(par, w, 2)[:, i, :],
                                      start=i == 0 and m == 0, stop=i == IC - 1 and m == 2)
                if pair == PAIRS - 1:
                    last.then_inc(s_down, 1)

            def tile(e, j, n):
                par = e % 2
                pe.wait_ge(s_xlo, n + 1)
                gate_up(par, 0, n)
                gate_up(par, 1, n)
                gate_up(par, 2, n)
                contract(par, 0, n)
                gate_up(par, 3, n)
                contract(par, 1, n)
                turn_rows(n * 16 + 32)
                contract(par, 2, n)
                contract(par, 3, n)

            turn_rows(16)
            over_tiles(pe, "pe_count", lambda e, n: pe.wait_ge(s_split, 3 * (e + 1)), tile)

        @block.scalar
        def _(act):
            def high_of_rows(done):
                act.wait_ge(s_turned, done)
                nc.scalar.activation(x_hi[:], turned[:], ACT.Copy).then_inc(s_xhi, 1)

            def tile(e, j, n):
                for pair in range(PAIRS):
                    act.wait_ge(s_pair, n * PAIRS + (pair + 1))
                    nc.scalar.activation(silu[pair % 2][:], gate[pair % 2][:], ACT.Silu).then_inc(s_silu, 1)
                    act.wait_ge(s_made, n * PAIRS + (pair + 3))
                    nc.scalar.activation(h_hi[:, 2 * pair:2 * pair + 2, :], h[pair % 2][:], ACT.Copy).then_inc(s_hhi, 1)
                high_of_rows(n + 2)

            high_of_rows(1)
            over_tiles(act, "act_count", lambda e, n: None, tile)
            act.wait_ge(s_all, 1)
            half = TOKENS // 2
            act.dma_start(out.rearrange("b s d -> (b s) d")[half:], acc[half:TOKENS]).then_inc(s_out, 16)

        @block.vector
        def _(dve):
            V = nc.vector

            def rest_of_rows(done):
                dve.wait_ge(s_xhi, done)
                V.tensor_tensor(x_lo[:], turned[:], x_hi[:].bitcast(fp32), ALU.subtract).then_inc(s_xlo, 1)

            def tile(e, j, n):
                for pair in range(PAIRS):
                    dve.wait_ge(s_silu, n * PAIRS + (pair + 1))
                    V.tensor_tensor(h[pair % 2][:], silu[pair % 2][:], up[pair % 2][:], ALU.mult).then_inc(s_made, 1)
                    dve.wait_ge(s_hhi, n * PAIRS + (pair + 1))
                    V.tensor_tensor(h_lo[:, 2 * pair:2 * pair + 2, :], h[pair % 2][:],
                                    h_hi[:, 2 * pair:2 * pair + 2, :].bitcast(fp32), ALU.subtract).then_inc(s_hlo, 1)
                    if pair == 1:
                        dve.wait_ge(s_added, n * (16 * TT))
                        V.tensor_copy(token[:], xg[:, :, TOKCOL].bitcast(i32))
                        V.tensor_copy(weight[:], xg[:, :, COMB + e]).then_inc(s_noted, 1)
                rest_of_rows(n + 2)
                dve.wait_ge(s_down, n + 1)
                for t in range(TT):
                    V.tensor_scalar(y[:, t, :], down[t][:, 0:D], weight[:, t:t + 1], None, ALU.mult).then_inc(s_y, 1)

            V.memset(note[:], 0.0).then_inc(s_made, 2)
            rest_of_rows(1)
            over_tiles(dve, "dve_count", lambda e, n: None, tile)

        @block.gpsimd
        def _(pool):
            alone = Alone(pool, "pool_awaited2", (s_split, 3))

            def before_expert(e, n):
                if e + 1 < EXPERTS:
                    alone.wait_ge(s_down, n)
                    split_weights(pool, e + 1, hi[(e + 1) % 2], lo[(e + 1) % 2])
                if e + 2 < EXPERTS:
                    load_stage(pool, e + 2)

            def tile(e, j, n):
                for t in range(TT):
                    pool.wait_ge(s_y, n * TT + (t + 1))
                    alone.wait_ge(s_added, n * (16 * TT) + 16 * t)
                    pool.indirect_dma_start(acc, bass.IndirectOffsetOnAxis(token[:, t:t + 1], axis=0),
                                            y[:, t, :], None, compute_op=ALU.add).then_inc(s_added, 16)

            total = over_tiles(pool, "pool_count", before_expert, tile)
            alone.wait_ge(s_added, total * (16 * TT))
            nc.gpsimd.memset(note[:, 0:1], 0.0).then_inc(s_all, 1)


def kernel(x, ctx_1024, g_xattn, g_ffn, L0_xattn_w_q, L0_xattn_b_q, L0_xattn_w_k, L0_xattn_b_k,
           L0_xattn_w_v, L0_xattn_b_v, L0_xattn_w_o, L0_xattn_b_o, L0_ffn_conf_w, L0_ffn_conf_b,
           L0_ffn_gate_w, L0_ffn_up_w, L0_ffn_down_w, L0_ffn_wealth):
    import numpy as np
    import concourse.bacc as bacc
    from concourse.bass_utils import run_bass_kernel_spmd

    def a(value):
        return np.asarray(value)

    def head_columns(w):
        wide = np.zeros((D, HEADS, SLOT), w.dtype)
        wide[:, :, :DK] = w.T.reshape(D, HEADS, DK)
        return wide.reshape(D, HEADS * SLOT)

    def head_rows(b, behind):
        wide = np.zeros((HEADS, SLOT), b.dtype)
        wide[:, :DK] = b.reshape(HEADS, DK)
        wide[:, DK] = behind
        return np.ascontiguousarray(wide.reshape(GROUPS, P).T)

    def on_partitions(row, repeat=1):
        return np.ascontiguousarray(np.broadcast_to(np.tile(row.reshape(-1), repeat), (P, row.size * repeat)))

    pad_rows = np.zeros((TILE, ROW), np.float32)
    pad_rows[:, TOKCOL] = np.arange(TOKENS, TOKENS + TILE, dtype=np.int32).view(np.float32)
    experts = np.arange(EXPERTS, dtype=np.float32)
    arrays = {
        "x": a(x),
        "ctxT": np.ascontiguousarray(a(ctx_1024).transpose(0, 2, 1)),
        "wq": head_columns(a(L0_xattn_w_q)),
        "wk": head_columns(a(L0_xattn_w_k)),
        "wv": np.ascontiguousarray(a(L0_xattn_w_v).T),
        "wo": np.ascontiguousarray(a(L0_xattn_w_o).T),
        "bq": head_rows(a(L0_xattn_b_q), 0),
        "bk": head_rows(a(L0_xattn_b_k), 1),
        "bv": on_partitions(a(L0_xattn_b_v)),
        "bo": on_partitions(a(L0_xattn_b_o)),
        "confT": np.ascontiguousarray(a(L0_ffn_conf_w).T),
        "conf_b": on_partitions(a(L0_ffn_conf_b), QT),
        "wealth": on_partitions(a(L0_ffn_wealth), QT),
        "g_attn": on_partitions(a(g_xattn)),
        "g_ffn": on_partitions(a(g_ffn)),
        "gate_T": np.ascontiguousarray(a(L0_ffn_gate_w).transpose(0, 2, 1)),
        "up_T": np.ascontiguousarray(a(L0_ffn_up_w).transpose(0, 2, 1)),
        "down_T": np.ascontiguousarray(a(L0_ffn_down_w).transpose(0, 2, 1)),
        "ident": np.eye(P, dtype=np.float32),
        "tri": np.triu(np.ones((P, P), np.float32), 1),
        "expert_row": on_partitions(experts * REGION, QT),
        "expert_no": on_partitions(experts, QT),
        "token_no": np.ascontiguousarray(np.arange(TOKENS, dtype=np.int32).reshape(-1, P).T),
        "pad_rows": pad_rows,
    }
    nc = bacc.Bacc("TRN2", target_bir_lowering=False, num_devices=1)
    handles = {name: nc.dram_tensor(name, list(v.shape), mybir.dt.from_np(v.dtype), kind="ExternalInput").ap()
               for name, v in arrays.items()}
    out = nc.dram_tensor("out", [BATCHES, SEQ, D], fp32, kind="ExternalOutput").ap()
    build_program(nc, out=out, **handles)
    result = run_bass_kernel_spmd(nc, [arrays], core_ids=[0])
    return result.results[0]["out"]
```

```python
import concourse.bass as bass
from concourse import mybir
from contextlib import ExitStack

BATCHES, SEQ, D = 16, 256, 256
HEADS, DK = 16, 16
EXPERTS, INNER = 8, 1024
P = 128
TOKENS = BATCHES * SEQ
HC = D // P
QT = SEQ // P
SLOT = 32
GROUPS = HEADS * SLOT // P
HPG = P // SLOT
STACK = 64
HPP = P // STACK
HPAIRS = HEADS // HPP
SHIFT = 3 * DK
TILE = 256
TT = TILE // P
REGION = TOKENS + TILE
ROW = 272
COMB = D
TOKCOL = D + EXPERTS
NCONST = 19
BLOCKS = P // DK // HPP
UNIT = HPAIRS + 4
IC = INNER // P
PAIRS = IC // 2
WCOLS = 3 * HC * INNER
EPS = 1e-5
FAR = -3.0e38

fp32 = mybir.dt.float32
f32r = mybir.dt.float32r
i32 = mybir.dt.int32
ALU = mybir.AluOpType
ACT = mybir.ActivationFunctionType
AX = mybir.AxisListType


def build_program(nc, x, ctxT, wq, wk, wv, wo, bq, bk, bv, bo, confT, conf_b, wealth, g_attn, g_ffn,
                  gate_T, up_T, down_T, ident, tri, expert_row, expert_no, token_no, ones_at, pick_rows, pad_rows, out):
    disp = nc.dram_tensor("dispatched", [EXPERTS * REGION, ROW], fp32, kind="Internal").ap()
    acc = nc.dram_tensor("accumulated", [TOKENS + P, D], fp32, kind="Internal").ap()

    with ExitStack() as keep:
        def sb(stack, name, shape, dt=fp32):
            return stack.enter_context(nc.sbuf_tensor(name, shape, dt))

        def sem(name):
            return keep.enter_context(nc.semaphore(name))

        stage = sb(keep, "stage", [P, WCOLS])
        idn = sb(keep, "idn", [P, P])
        counts = sb(keep, "counts", [P, EXPERTS], i32)
        tiles = sb(keep, "tiles", [P, EXPERTS], i32)

        s_stage = [sem(f"stage_loaded{n}") for n in range(3)]
        s_split = sem("weights_split")
        s_hi = sem("weights_hi")

        third = WCOLS // 3

        def load_third(eng, e, n):
            of = (gate_T, up_T, down_T)[n][e].rearrange("(c p) n -> p c n", p=P)
            eng.dma_start(stage[:, n * third:(n + 1) * third].rearrange("p (c n) -> p c n", c=of.shape[1]),
                          of).then_inc(s_stage[n], 16)

        def high_third(eng, e, n, hi):
            eng.wait_ge(s_stage[n], 16 * (e + 1))
            part = slice(n * third, (n + 1) * third)
            nc.scalar.activation(hi[:, part], stage[:, part], ACT.Copy).then_inc(s_hi, 1)

        def rest_third(eng, e, n, hi, lo):
            eng.wait_ge(s_hi, 3 * e + n + 1)
            part = slice(n * third, (n + 1) * third)
            eng.tensor_tensor(lo[:, part], stage[:, part], hi[:, part].bitcast(fp32), ALU.subtract).then_inc(s_split, 1)

        attention_stage(nc, sb, sem, load_third, disp, acc, x, ctxT, wq, wk, wv, wo,
                        bq, bk, bv, bo, confT, conf_b, wealth, g_attn, g_ffn, ident, tri,
                        expert_row, expert_no, token_no, ones_at, pick_rows, pad_rows, idn, counts, tiles)
        expert_stage(nc, sb, sem, load_third, high_third, rest_third, disp, acc, idn, tiles,
                     s_split, out)


class Alone:

    def __init__(self, eng, name, seen):
        self.eng, self.seen, self.register = eng, seen, eng.alloc_register(name)

    def wait_ge(self, semaphore, value):
        if not isinstance(value, int):
            self.eng.reg_mov(self.register, value)
            value = self.register
        self.eng.wait_ge(*self.seen)
        self.eng.wait_ge(semaphore, value)


def attention_stage(nc, sb_in, sem, load_third, disp, acc, x, ctxT, wq, wk, wv, wo,
                    bq, bk, bv, bo, confT, conf_b, wealth, g_attn, g_ffn, ident, tri,
                    expert_row, expert_no, token_no, ones_at, pick_rows, pad_rows, idn, counts, tiles):
    with ExitStack() as own:
        def sb(name, shape, dt=fp32):
            return sb_in(own, name, shape, dt)

        x_all = sb("x_all", [P, BATCHES, QT, D])
        cT = [sb(f"ctxT{i}", [P, HC, SEQ]) for i in range(2)]
        wq_s = sb("wq_s", [P, HC, D])
        wk_s = sb("wk_s", [P, HC, D])
        wv_s = sb("wv_s", [P, HC, D])
        wo_s = sb("wo_s", [P, HC, D])
        bq_s = sb("bq_s", [P, HC])
        bk_s = sb("bk_s", [P, HC])
        bv_s = sb("bv_s", [P, D])
        bo_s = sb("bo_s", [P, D])
        conf_s = sb("conf_s", [P, HC, EXPERTS])
        cb_s = sb("cb_s", [P, QT, EXPERTS])
        wealth_s = sb("wealth_s", [P, QT, EXPERTS])
        eoff = sb("eoff", [P, QT, EXPERTS])
        eno = sb("eno", [P, QT, EXPERTS])
        tok = sb("tok", [P, BATCHES * QT], i32)
        tri_s = sb("tri_s", [P, P])
        ones = sb("ones", [P, P])
        pads = sb("pads", [P, ROW])
        gates = sb("gates", [P, 2])
        tg = sb("tg", [P, 2])
        minus_half = sb("minus_half", [P, QT])
        stats = sb("stats", [P, QT, 6])
        mv = sb("mv", [P, QT, 2])
        rstd = sb("rstd", [P, QT])
        shift = sb("shift", [P, QT])
        stats2 = sb("stats2", [P, QT, 6])
        mv2 = sb("mv2", [P, QT, 2])
        rstd2 = sb("rstd2", [P, QT])
        shift2 = sb("shift2", [P, QT])
        xn = sb("xn", [P, QT, D])
        xT = sb("xT", [P, HC, SEQ])
        dense = {what: sb(f"{what}_dense", [P, HC, SEQ]) for what in "QK"}
        high = {what: sb(f"{what}_high", [P, HC, SEQ], f32r) for what in "QK"}
        rest = {what: sb(f"{what}_rest", [P, HC, SEQ], f32r) for what in "QK"}
        q = [sb(f"queries{i}", [P, HPAIRS, SEQ], f32r) for i in range(2)]
        k = [sb(f"keys{i}", [P, HPAIRS, SEQ], f32r) for i in range(2)]
        picks = {what: sb(f"picks_{what}", [P, BLOCKS, P], f32r) for what in ("Q high", "Q rest", "K high", "K rest")}
        ones_row = sb("ones_row", [P, 1])
        max_neg = sb("max_neg", [P, QT, HEADS])
        max_rows = sb("max_rows", [HEADS, SEQ], f32r)
        v = [sb(f"values{i}", [P, QT, HEADS, SLOT]) for i in range(2)]
        probs = [sb(f"probs{i}", [P, HPG, QT, SEQ]) for i in range(2)]
        oS = sb("oS", [P, GROUPS, SEQ])
        rsum = sb("rsum", [P, QT, HEADS])
        on = sb("on", [P, QT, D])
        oT = sb("oT", [P, HC, SEQ])
        row = sb("row", [P, QT, ROW])
        x2T = sb("x2T", [P, HC, SEQ])
        z = sb("z", [P, QT, EXPERTS])
        ez = sb("ez", [P, QT, EXPERTS])
        bids = sb("bids", [P, QT, EXPERTS])
        t8 = sb("t8", [P, QT, EXPERTS])
        u8 = sb("u8", [P, QT, EXPERTS])
        bqs = sb("bqs", [P, HC])
        m1 = sb("m1", [P, QT, EXPERTS])
        m2 = sb("m2", [P, QT, EXPERTS])
        m12 = sb("m12", [P, QT, EXPERTS])
        macc = sb("macc", [P, EXPERTS])
        v1 = sb("v1", [P, QT])
        v2 = sb("v2", [P, QT])
        r1 = sb("r1", [P, QT])
        dv = sb("dv", [P, QT])
        ed = sb("ed", [P, QT])
        w1 = sb("w1", [P, QT])
        c8 = sb("c8", [P, QT, EXPERTS])
        w2 = sb("w2", [P, QT])
        posf = sb("posf", [P, 2, QT])
        posi = sb("posi", [P, 2, QT], i32)

        scores = own.enter_context(nc.psum_tensor("scores", [P, 2, HPP * QT, SEQ], fp32))
        maxps = own.enter_context(nc.psum_tensor("maxps", [P, 2, QT, SEQ], fp32))
        pv = own.enter_context(nc.psum_tensor("pv", [P, 512], fp32))
        misc = own.enter_context(nc.psum_tensor("misc", [P, 2, 256], fp32))


        names = """x_loaded ctx_loaded consts_loaded pads_loaded pads_stored consts_made constants_ready
            misc_written misc_read ln_stats ln_chain ln_scaled ln_done ln2_chain ln2_stats ln2_scaled
            ln2_done bias_added q_split k_split high_chain unit_written unit_read picks_loaded shifted max_scored max_taken pv_done pv_read
            sums_inverted x2_stored sigmoid_half_ready route_chain masks_ready second_ready
            rows_chain rows_ready scattered counts_summed count_chain counted values_made
            scale_chain scale2_chain""".split()
        s = {n: sem(n) for n in names}

        AHEAD, NEXT, BACK = ["K", "TX", "Q"], ["V", "MT"], ["TO0", "TO1", "TN", "WO", "TX2", "LG", "RK"]
        FULL = ["V", "TO0", "TO1", "TN", "K", "TX", "WO", "Q", "TX2", "LG", "MT", "RK"]

        class Use:

            def __init__(self, order, before):
                self.order, self.before = order, before

            def free(self, eng, what):
                n = self.before + self.order.index(what)
                if not (isinstance(n, int) and n == 0):
                    eng.wait_ge(s["misc_read"], n)

            def after(self, what):
                return self.before + (self.order.index(what) + 1)

            def written(self, eng, what):
                eng.wait_ge(s["misc_written"], self.after(what))

            def read(self, eng, what):
                eng.wait_ge(s["misc_read"], self.after(what))

        def first_unit(b):
            last = isinstance(b, int) and b == BATCHES - 1
            return b * UNIT + 8 if not last else b * UNIT + 4

        def after_all(use):
            return use.before + len(use.order)

        PRO0 = Use(AHEAD, 0)
        PRO1 = Use(AHEAD, after_all(PRO0))
        PRO2 = Use(NEXT, after_all(PRO1))
        ITER0 = Use([n for n in FULL if n not in BACK], after_all(PRO2))
        before1 = after_all(ITER0)

        def full_use(b):
            return Use(FULL, b * len(FULL) + (before1 - len(FULL)))

        ITER14 = Use([n for n in FULL if n not in AHEAD], after_all(full_use(BATCHES - 3)))
        ITER15 = Use(BACK, after_all(ITER14))
        EPILOGUE = Use(BACK, after_all(ITER15))

        def over_batches(eng, body):
            body(0, 0, ITER0, True, True, False)
            with eng.Fori(0, BATCHES // 2 - 2) as i:
                for b, par in ((i * 2 + 1, 1), (i * 2 + 2, 0)):
                    body(b, par, full_use(b), True, True, True)
            body(BATCHES - 3, 1, full_use(BATCHES - 3), True, True, True)
            body(BATCHES - 2, 0, ITER14, False, True, True)
            body(BATCHES - 1, 1, ITER15, False, False, True)

        def of_batch(b, t):
            return x_all[:, bass.ds(b, 1), t, :].rearrange("p o d -> p (o d)")

        def is_first(b):
            return isinstance(b, int) and b == 0

        def chain(eng, name, each, b):
            n = [0]

            def link(instruction):
                n[0] += 1
                assert n[0] <= each
                instruction.then_inc(s[name], 1)
                eng.wait_ge(s[name], b * each + n[0])
            return link

        block = own.enter_context(nc.Block())

        @block.sync
        def _(sp):
            def load_x(b):
                sp.dma_start(x_all[:, b], x[b].rearrange("(t p) d -> p t d", p=P)).then_inc(s["x_loaded"], 16)

            load_x(0)
            sp.dma_start(probs[0][:], pick_rows).then_inc(s["picks_loaded"], 16)
            sp.dma_start(cT[0][:], ctxT[0].rearrange("(c p) s -> p c s", p=P)).then_inc(s["ctx_loaded"], 16)
            consts = ((idn[:], ident), (wq_s[:], wq.rearrange("(c p) n -> p c n", p=P)), (bq_s[:], bq),
                      (wk_s[:], wk.rearrange("(c p) n -> p c n", p=P)), (bk_s[:], bk),
                      (wv_s[:], wv.rearrange("(c p) n -> p c n", p=P)), (bv_s[:], bv),
                      (gates[:, 0:1], g_attn), (gates[:, 1:2], g_ffn), (bo_s[:], bo),
                      (wo_s[:], wo.rearrange("(c p) n -> p c n", p=P)),
                      (conf_s[:], confT.rearrange("(c p) n -> p c n", p=P)), (cb_s[:], conf_b),
                      (wealth_s[:], wealth), (eoff[:], expert_row), (eno[:], expert_no),
                      (tri_s[:], tri), (tok[:], token_no), (ones_row[:], ones_at))
            assert len(consts) == NCONST
            for to, of in consts:
                sp.dma_start(to, of).then_inc(s["consts_loaded"], 16)
            sp.dma_start(pads[:], pad_rows).then_inc(s["pads_loaded"], 16)

            def load_ctx(b, par):
                sp.wait_ge(s["ctx_loaded"], b * 16)
                sp.dma_start(cT[par][:], ctxT[bass.ds(b, 1)].rearrange("o (c p) s -> p (o c) s", p=P)).then_inc(s["ctx_loaded"], 16)

            load_ctx(1, 1)
            sp.wait_ge(s["x_loaded"], 16)
            load_x(1)

            def store_shift(b, par, use):
                use.read(sp, "MT")
                for u in range(HPP):
                    row_ = u * STACK + SHIFT
                    sp.dma_start(q[par][row_:row_ + 1].bitcast(fp32), max_rows[u * HPAIRS:(u + 1) * HPAIRS].bitcast(fp32)).then_inc(s["shifted"], 16)

            for b in range(2, BATCHES):
                sp.wait_ge(s["x_loaded"], 16 * b)
                load_x(b)
            PRO2.read(sp, "V")
            load_ctx(2, 0)
            store_shift(0, 0, PRO2)
            sp.wait_ge(s["pads_loaded"], 16)
            sp.dma_start(acc[TOKENS:], pads[:, 0:D]).then_inc(s["pads_stored"], 16)

            def store_residual(b, use):
                use.read(sp, "WO")
                sp.dma_start(acc[bass.ds(b * SEQ, SEQ)].rearrange("(t p) d -> p t d", p=P),
                             x_all[:, bass.ds(b, 1)].rearrange("p o t d -> p (o t) d")).then_inc(s["x2_stored"], 16)

            def body(b, par, use, ahead, nxt, back):
                if ahead and not (isinstance(b, int) and b + 3 >= BATCHES):
                    use.read(sp, "V")
                    load_ctx(b + 3, 1 - par)
                if back:
                    store_residual(b - 1, use)
                if nxt:
                    store_shift(b + 1, 1 - par, use)

            over_batches(sp, body)
            store_residual(BATCHES - 1, EPILOGUE)
            sp.wait_ge(s["counted"], 1)
            for e in range(EXPERTS):
                n = sp.value_load(counts[0:1, e:e + 1], min_val=0, max_val=TOKENS)
                sp.dma_start(disp[bass.ds(n + e * REGION, TILE)].rearrange("(t p) d -> p t d", p=P),
                             pads[:].unsqueeze(1).to_broadcast([P, TT, ROW])).then_inc(s["pads_stored"], 16)
            sp.wait_ge(s["x2_stored"], 16 * BATCHES)
            sp.wait_ge(s["pads_stored"], 16 + 16 * EXPERTS)

        @block.tensor
        def _(pe):
            mm = nc.tensor.matmul

            def turn(source, what, use):
                use.free(pe, what)
                for t in range(QT):
                    for c in range(HC):
                        last = nc.tensor.transpose(misc[:, c, t * P:(t + 1) * P], source[:, t, c * P:(c + 1) * P], idn[:])
                last.then_inc(s["misc_written"], 1)

            def turn_x(b, use):
                pe.wait_ge(s["ln_done"], b * QT + QT)
                turn(xn, "TX", use)

            def project(weights, source, what, use):
                use.free(pe, what)
                for o in range(HC):
                    for c in range(HC):
                        last = mm(misc[:, o, :], weights[:, c, o * P:(o + 1) * P], source[:, c, :], start=c == 0, stop=c == HC - 1)
                last.then_inc(s["misc_written"], 1)

            def project_q(use):
                use.read(pe, "TX")
                project(wq_s, xT, "Q", use)

            def project_k(b, par, use):
                pe.wait_ge(s["ctx_loaded"], b * 16 + 16)
                project(wk_s, cT[par], "K", use)

            def project_v(par, use):
                use.free(pe, "V")
                for t in range(QT):
                    for c in range(HC):
                        last = mm(misc[:, t, :], cT[par][:, c, t * P:(t + 1) * P], wv_s[:, c, :], start=c == 0, stop=c == HC - 1)
                last.then_inc(s["misc_written"], 1)

            def write_unit(n):
                if not (isinstance(n, int) and n < 2):
                    pe.wait_ge(s["unit_read"], n - 1)

            def stack(b, what, unit):
                for c in range(HC):
                    if c == 0:
                        pe.wait_ge(s["q_split" if what == "Q" else "k_split"], b + 1)
                    write_unit(unit + c)
                    for i in range(BLOCKS):
                        mm(scores[:, c, i, :], picks[what + " high"][:, i, :], high[what][:, c, :], start=True, stop=False)
                        last = mm(scores[:, c, i, :], picks[what + " rest"][:, i, :], rest[what][:, c, :], start=False, stop=True)
                    last.then_inc(s["unit_written"], 1)

            def max_scores(b, par, pair, units):
                if pair == 0:
                    pe.wait_ge(s["unit_read"], units)
                if not (is_first(b) and pair == 0):
                    pe.wait_ge(s["max_taken"], b * HPAIRS + pair)
                for t in range(QT):
                    for u in range(HPP):
                        r = slice(u * STACK, u * STACK + SHIFT)
                        last = mm(maxps[:, u, t, :], q[par][r, pair, t * P:(t + 1) * P], k[par][r, pair, :], start=True, stop=True)
                last.then_inc(s["max_scored"], 1)

            def turn_maxima(b, use):
                pe.wait_ge(s["max_taken"], b * HPAIRS + HPAIRS)
                use.free(pe, "MT")
                for t in range(QT):
                    last = nc.tensor.transpose(misc[0:HEADS, 0, t * P:(t + 1) * P], max_neg[:, t, :], idn[:])
                last.then_inc(s["misc_written"], 1)

            def score(b, par, pair):
                if pair == 0:
                    pe.wait_ge(s["shifted"], b * (16 * HPP) + 16 * HPP)
                write_unit(first_unit(b) + pair)
                for t in range(QT):
                    for u in range(HPP):
                        r = slice(u * STACK, (u + 1) * STACK)
                        last = mm(scores[:, pair % 2, u * QT + t, :], k[par][r, pair, t * P:(t + 1) * P], q[par][r, pair, :],
                                  start=True, stop=True)
                last.then_inc(s["unit_written"], 1)

            def weigh(b, par, g):
                pe.wait_ge(s["unit_read"], first_unit(b) + (2 * g + 2))
                if not (is_first(b) and g == 0):
                    pe.wait_ge(s["pv_read"], b * GROUPS + g)
                for t in range(QT):
                    for j in range(HPG):
                        last = mm(pv[j * SLOT:(j + 1) * SLOT, 0:SEQ], v[par][:, t, g * HPG + j, :], probs[g % 2][:, j, t, :],
                                  start=t == 0, stop=t == QT - 1)
                last.then_inc(s["pv_done"], 1)

            def turn_heads(b, t, use):
                if t == 0:
                    pe.wait_ge(s["pv_read"], b * GROUPS + GROUPS)
                use.free(pe, f"TO{t}")
                for g in range(GROUPS):
                    last = nc.tensor.transpose(misc[:, g // 2, (g % 2) * P:(g % 2 + 1) * P], oS[:, g, t * P:(t + 1) * P], idn[:])
                last.then_inc(s["misc_written"], 1)

            def turn_normed(use):
                use.read(pe, "TO1")
                turn(on, "TN", use)

            def attn_out(use):
                use.read(pe, "TN")
                use.free(pe, "WO")
                for t in range(QT):
                    for c in range(HC):
                        last = mm(misc[:, t, :], oT[:, c, t * P:(t + 1) * P], wo_s[:, c, :], start=c == 0, stop=c == HC - 1)
                last.then_inc(s["misc_written"], 1)

            def turn_x2(b, use):
                pe.wait_ge(s["ln2_done"], b * QT + QT)
                turn(row, "TX2", use)

            def logits(use):
                use.read(pe, "TX2")
                use.free(pe, "LG")
                for t in range(QT):
                    for c in range(HC):
                        last = mm(misc[:, t, 0:EXPERTS], x2T[:, c, t * P:(t + 1) * P], conf_s[:, c, :], start=c == 0, stop=c == HC - 1)
                last.then_inc(s["misc_written"], 1)

            def ranks(b, use):
                pe.wait_ge(s["masks_ready"], b + 1)
                use.free(pe, "RK")
                for t in range(QT):
                    mm(misc[:, t, 0:EXPERTS], tri_s[:], m12[:, t, :], start=True, stop=False)
                    if t == 1:
                        mm(misc[:, t, 0:EXPERTS], ones[:], m12[:, 0, :], start=False, stop=False)
                    last = mm(misc[:, t, 0:EXPERTS], ones[:], macc[:], start=False, stop=True)
                last.then_inc(s["misc_written"], 1)

            pe.wait_ge(s["consts_loaded"], 16 * NCONST)
            pe.wait_ge(s["constants_ready"], 1)
            for b, use in ((0, PRO0), (1, PRO1)):
                project_k(b, b, use)
                turn_x(b, use)
                project_q(use)
                stack(b, "K", 4 * b)
                stack(b, "Q", 4 * b + 2)
            project_v(0, PRO2)
            for pair in range(HPAIRS):
                max_scores(0, 0, pair, 4)
            turn_maxima(0, PRO2)

            def body(b, par, use, ahead, nxt, back):
                def max_of_next(pair):
                    if nxt:
                        max_scores(b + 1, 1 - par, pair, first_unit(b))

                score(b, par, 0)
                if nxt:
                    project_v(1 - par, use)
                max_of_next(0)
                score(b, par, 1)
                if back:
                    turn_heads(b - 1, 0, use)
                max_of_next(1)
                if back:
                    turn_heads(b - 1, 1, use)
                score(b, par, 2)
                if back:
                    turn_normed(use)
                max_of_next(2)
                if ahead:
                    project_k(b + 2, par, use)
                score(b, par, 3)
                weigh(b, par, 0)
                if ahead:
                    turn_x(b + 2, use)
                max_of_next(3)
                score(b, par, 4)
                if back:
                    attn_out(use)
                max_of_next(4)
                score(b, par, 5)
                if ahead:
                    project_q(use)
                weigh(b, par, 1)
                max_of_next(5)
                score(b, par, 6)
                if back:
                    turn_x2(b - 1, use)
                max_of_next(6)
                score(b, par, 7)
                max_of_next(7)
                weigh(b, par, 2)
                if back:
                    logits(use)
                if nxt:
                    turn_maxima(b + 1, use)
                if ahead:
                    stack(b + 2, "K", first_unit(b) + HPAIRS)
                weigh(b, par, 3)
                if ahead:
                    stack(b + 2, "Q", first_unit(b) + (HPAIRS + 2))
                if back:
                    ranks(b - 1, use)

            over_batches(pe, body)
            last_batch = BATCHES - 1
            turn_heads(last_batch, 0, EPILOGUE)
            turn_heads(last_batch, 1, EPILOGUE)
            turn_normed(EPILOGUE)
            attn_out(EPILOGUE)
            turn_x2(last_batch, EPILOGUE)
            logits(EPILOGUE)
            ranks(last_batch, EPILOGUE)
            pe.wait_ge(s["counts_summed"], 2 * BATCHES)
            mm(misc[:, 0, 0:EXPERTS], ones[:], macc[:], start=True, stop=True).then_inc(s["misc_written"], 1)

        @block.scalar
        def _(act):
            def exps(b, pair):
                act.wait_ge(s["unit_written"], first_unit(b) + (pair + 1))
                g = pair // 2
                if not (is_first(b) and g < 2):
                    act.wait_ge(s["pv_done"], b * GROUPS + (g - 1))
                at = pair % 2 * HPP
                nc.scalar.activation(probs[g % 2][:, at:at + HPP].rearrange("p u t s -> p (u t) s"), scores[:, pair % 2],
                                     ACT.Exp).then_inc(s["unit_read"], 1)

            def read_stack(par, what, unit):
                to, bias = (q, 0.0) if what == "Q" else (k, ones_row[:, 0:1])
                for c in range(HC):
                    act.wait_ge(s["unit_written"], unit + (c + 1))
                    nc.scalar.activation(to[par][:, c * BLOCKS:(c + 1) * BLOCKS, :], scores[:, c], ACT.Identity,
                                         bias=bias).then_inc(s["unit_read"], 1)

            def norm_x(b):
                act.wait_ge(s["ln_scaled"], b + 1)
                for t in range(QT):
                    nc.scalar.activation(xn[:, t, :], of_batch(b, t), ACT.Identity,
                                         bias=shift[:, t:t + 1], scale=rstd[:, t:t + 1]).then_inc(s["ln_done"], 1)

            def norm_x2(b):
                act.wait_ge(s["ln2_scaled"], b + 1)
                if not is_first(b):
                    act.wait_ge(s["scattered"], b * (16 * 2 * QT))
                for t in range(QT):
                    nc.scalar.activation(row[:, t, 0:D], of_batch(b, t), ACT.Identity, bias=shift2[:, t:t + 1],
                                         scale=rstd2[:, t:t + 1]).then_inc(s["ln2_done"], 1)

            def read_whole(to, what, use):
                use.written(act, what)
                nc.scalar.activation(to, misc[:], ACT.Copy).then_inc(s["misc_read"], 1)

            def read_dense(b, what, bias, scale, use):
                use.written(act, what)
                if not is_first(b):
                    act.wait_ge(s["q_split" if what == "Q" else "k_split"], b)
                for c in range(HC):
                    last = nc.scalar.activation(dense[what][:, c, :], misc[:, c, :], ACT.Identity, bias=bias[:, c:c + 1], scale=scale)
                last.then_inc(s["misc_read"], 1)

            def read_q(b, use):
                read_dense(b, "Q", bqs, DK ** -0.5, use)

            def read_k(b, use):
                read_dense(b, "K", bk_s, 1.0, use)

            def read_pv(b, g):
                act.wait_ge(s["pv_done"], b * GROUPS + (g + 1))
                nc.scalar.activation(oS[:, g, :], pv[:, 0:SEQ], ACT.Copy).then_inc(s["pv_read"], 1)

            def sigmoid(use):
                use.read(act, "LG")
                nc.scalar.activation(ez[:], z[:], ACT.Exp, scale=-1.0).then_inc(s["sigmoid_half_ready"], 1)

            def second_weight(b):
                act.wait_ge(s["masks_ready"], b + 1)
                nc.scalar.activation(ed[:], dv[:], ACT.Exp).then_inc(s["second_ready"], 1)

            act.wait_ge(s["consts_loaded"], 16 * NCONST)
            nc.scalar.activation(tg[:], gates[:], ACT.Tanh).then_inc(s["consts_made"], 1)
            nc.scalar.activation(bqs[:], bq_s[:], ACT.Copy, scale=DK ** -0.5).then_inc(s["consts_made"], 1)
            act.wait_ge(s["consts_made"], 2)
            for b, use in ((0, PRO0), (1, PRO1)):
                read_k(b, use)
                norm_x(b)
                read_whole(xT[:], "TX", use)
                read_q(b, use)
                read_stack(b, "K", 4 * b)
                read_stack(b, "Q", 4 * b + 2)

            def body(b, par, use, ahead, nxt, back):
                exps(b, 0)
                exps(b, 1)
                exps(b, 2)
                if back:
                    read_whole(oT[:], "TN", use)
                if ahead:
                    read_k(b + 2, use)
                exps(b, 3)
                if ahead:
                    norm_x(b + 2)
                read_pv(b, 0)
                if ahead:
                    read_whole(xT[:], "TX", use)
                exps(b, 4)
                exps(b, 5)
                if ahead:
                    read_q(b + 2, use)
                read_pv(b, 1)
                if back:
                    norm_x2(b - 1)
                exps(b, 6)
                if back:
                    read_whole(x2T[:], "TX2", use)
                exps(b, 7)
                read_pv(b, 2)
                if back:
                    sigmoid(use)
                if ahead:
                    read_stack(par, "K", first_unit(b) + HPAIRS)
                read_pv(b, 3)
                if back:
                    second_weight(b - 1)
                if ahead:
                    read_stack(par, "Q", first_unit(b) + (HPAIRS + 2))

            over_batches(act, body)
            read_whole(oT[:], "TN", EPILOGUE)
            norm_x2(BATCHES - 1)
            read_whole(x2T[:], "TX2", EPILOGUE)
            sigmoid(EPILOGUE)
            second_weight(BATCHES - 1)

        @block.vector
        def _(dve):
            V = nc.vector
            alone = Alone(dve, "dve_awaited", (s["consts_made"], 2))
            both8 = [P, QT, EXPERTS]

            def spread(column):
                return column[:].unsqueeze(2).to_broadcast(both8)

            def stats_x(b):
                alone.wait_ge(s["x_loaded"], b * 16 + 16)
                if not is_first(b):
                    alone.wait_ge(s["ln_stats"], b)
                link = chain(alone, "ln_chain", QT, b)
                for t in range(QT):
                    link(V.bn_stats(stats[:, t, :], of_batch(b, t)))
                if not is_first(b):
                    alone.wait_ge(s["ln_done"], b * QT)
                for t in range(QT):
                    last = V.bn_aggr(mv[:, t, :], stats[:, t, :])
                last.then_inc(s["ln_stats"], 1)

            def norm_heads(b, t, use):
                use.written(dve, f"TO{t}")
                heads = misc[:].rearrange("p a (h c) -> p (a h) c", c=SLOT)
                V.reciprocal(rsum[:, t, :], heads[:, :, DK]).then_inc(s["sums_inverted"], 1)
                dve.wait_ge(s["sums_inverted"], b * QT + (t + 1))
                V.tensor_tensor(on[:, t, :].rearrange("p (h d) -> p h d", d=DK), heads[:, :, 0:DK],
                                rsum[:, t, :].unsqueeze(2).to_broadcast([P, HEADS, DK]), ALU.mult).then_inc(s["misc_read"], 1)

            def residual(b, use):
                use.written(dve, "WO")
                dve.wait_ge(s["bias_added"], b + 1)
                if not is_first(b):
                    dve.wait_ge(s["ln2_done"], b * QT)
                xb = x_all[:, bass.ds(b, 1)].rearrange("p o t d -> p (o t d)")
                V.scalar_tensor_tensor(xb, misc[:].rearrange("p t d -> p (t d)"), tg[:, 0:1], xb,
                                       ALU.mult, ALU.add).then_inc(s["misc_read"], 1)
                use.read(alone, "WO")
                link = chain(alone, "ln2_chain", QT, b)
                for t in range(QT):
                    link(V.bn_stats(stats2[:, t, :], of_batch(b, t)))
                for t in range(QT):
                    last = V.bn_aggr(mv2[:, t, :], stats2[:, t, :])
                last.then_inc(s["ln2_stats"], 1)

            def read_v(par, use):
                use.written(dve, "V")
                for t in range(QT):
                    last = V.tensor_tensor(v[par][:, t, :, 0:DK], misc[:, t, :].rearrange("p (h d) -> p h d", d=DK),
                                           bv_s[:].rearrange("p (h d) -> p h d", d=DK), ALU.add)
                last.then_inc(s["misc_read"], 1)

            def maxima(b, pair):
                dve.wait_ge(s["max_scored"], b * HPAIRS + (pair + 1))
                to = max_neg[:].rearrange("p t (u n) -> p u t n", u=HPP)[:, :, :, pair]
                V.tensor_reduce(to, maxps[:], AX.X, ALU.max, negate=True).then_inc(s["max_taken"], 1)

            def read_maxima(b, use):
                use.written(dve, "MT")
                if not is_first(b):
                    dve.wait_ge(s["shifted"], b * (16 * HPP))
                V.tensor_copy(max_rows[:], misc[0:HEADS, 0, :]).then_inc(s["misc_read"], 1)

            def read_logits(b, use):
                use.written(dve, "LG")
                V.tensor_tensor(z[:], misc[:, :, 0:EXPERTS], cb_s[:], ALU.add).then_inc(s["misc_read"], 1)

            def top_two(b):
                dve.wait_ge(s["sigmoid_half_ready"], b + 1)
                link = chain(dve, "route_chain", 14, b)
                link(V.tensor_scalar(t8[:], ez[:], 1.0, None, ALU.add))
                link(V.reciprocal(u8[:], t8[:]))
                link(V.tensor_tensor(bids[:], u8[:], wealth_s[:], ALU.mult))
                link(V.tensor_reduce(v1[:], bids[:], AX.X, ALU.max))
                link(V.tensor_tensor(t8[:], bids[:], spread(v1), ALU.is_equal))
                link(V.scalar_tensor_tensor(u8[:], t8[:], -float(EXPERTS), eno[:], ALU.mult, ALU.add))
                link(V.tensor_reduce(r1[:], u8[:], AX.X, ALU.min))
                link(V.tensor_tensor(m1[:], u8[:], spread(r1), ALU.is_equal))
                link(V.scalar_tensor_tensor(bids[:], m1[:], FAR, bids[:], ALU.mult, ALU.add))
                link(V.tensor_reduce(v2[:], bids[:], AX.X, ALU.max))
                V.tensor_tensor(dv[:], v2[:], v1[:], ALU.subtract)
                link(V.tensor_tensor(t8[:], bids[:], spread(v2), ALU.is_equal))
                link(V.scalar_tensor_tensor(u8[:], t8[:], -float(EXPERTS), eno[:], ALU.mult, ALU.add))
                link(V.tensor_reduce(r1[:], u8[:], AX.X, ALU.min))
                link(V.tensor_tensor(m2[:], u8[:], spread(r1), ALU.is_equal))
                V.tensor_tensor(m12[:], m1[:], m2[:], ALU.add).then_inc(s["masks_ready"], 1)

            def positions(b, use):
                use.written(dve, "RK")
                V.tensor_tensor(u8[:], misc[:, :, 0:EXPERTS], eoff[:], ALU.add).then_inc(s["misc_read"], 1)
                for t in range(QT):
                    V.tensor_tensor(macc[:], macc[:], m12[:, t, :], ALU.add).then_inc(s["counts_summed"], 1)
                    dve.wait_ge(s["counts_summed"], b * QT + (t + 1))
                link = chain(dve, "rows_chain", 11, b)
                link(V.tensor_tensor(t8[:], m1[:], u8[:], ALU.mult))
                link(V.tensor_reduce(posf[:, 0, :], t8[:], AX.X, ALU.add))
                link(V.tensor_tensor(t8[:], m2[:], u8[:], ALU.mult))
                link(V.tensor_reduce(posf[:, 1, :], t8[:], AX.X, ALU.add))
                V.tensor_copy(posi[:], posf[:])
                dve.wait_ge(s["second_ready"], b + 1)
                link(V.tensor_scalar(w2[:], ed[:], 1.0, None, ALU.add))
                link(V.reciprocal(w1[:], w2[:]))
                link(V.tensor_scalar(w1[:], w1[:], tg[:, 1:2], None, ALU.mult))
                link(V.tensor_tensor(w2[:], w1[:], ed[:], ALU.mult))
                link(V.tensor_tensor(t8[:], m1[:], spread(w1), ALU.mult))
                link(V.tensor_tensor(c8[:], m2[:], spread(w2), ALU.mult))
                link(V.tensor_copy(row[:, :, TOKCOL:TOKCOL + 1].bitcast(i32),
                                   tok[:, bass.ds(b * QT, QT)].unsqueeze(2)))
                V.tensor_tensor(row[:, :, COMB:COMB + EXPERTS], t8[:], c8[:], ALU.add).then_inc(s["rows_ready"], 1)

            dve.wait_ge(s["picks_loaded"], 16)
            loaded = probs[0][:].rearrange("p m t (h c) -> p m (t h) c", c=P)
            for n, what in enumerate("QK"):
                for m, part in enumerate(("high", "rest")):
                    V.tensor_copy(picks[f"{what} {part}"][:], loaded[:, 2 * n + m])
            V.memset(v[0][:], 1.0)
            V.memset(v[1][:], 1.0)
            V.memset(macc[:], 0.0)
            V.memset(row[:, :, D:], 0.0)
            V.memset(minus_half[:], -0.5)
            V.memset(ones[:], 1.0).then_inc(s["constants_ready"], 1)
            dve.wait_ge(s["constants_ready"], 1)
            dve.wait_ge(s["consts_loaded"], 16 * NCONST)
            dve.wait_ge(s["consts_made"], 2)
            stats_x(0)
            stats_x(1)
            read_v(0, PRO2)
            for pair in range(HPAIRS):
                maxima(0, pair)
            read_maxima(0, PRO2)

            def body(b, par, use, ahead, nxt, back):
                def maxima_of_next(*pairs):
                    if nxt:
                        for pair in pairs:
                            maxima(b + 1, pair)

                if ahead:
                    stats_x(b + 2)
                if nxt:
                    read_v(1 - par, use)
                maxima_of_next(0)
                if back:
                    norm_heads(b - 1, 0, use)
                maxima_of_next(1)
                if back:
                    norm_heads(b - 1, 1, use)
                maxima_of_next(2, 3)
                if back:
                    residual(b - 1, use)
                maxima_of_next(4, 5, 6, 7)
                if back:
                    read_logits(b - 1, use)
                if nxt:
                    read_maxima(b + 1, use)
                if back:
                    top_two(b - 1)
                    positions(b - 1, use)

            over_batches(dve, body)
            b = BATCHES - 1
            norm_heads(b, 0, EPILOGUE)
            norm_heads(b, 1, EPILOGUE)
            residual(b, EPILOGUE)
            read_logits(b, EPILOGUE)
            top_two(b)
            positions(b, EPILOGUE)
            dve.wait_ge(s["misc_written"], EPILOGUE.before + len(BACK) + 1)
            link = chain(dve, "count_chain", 4, 0)
            link(V.tensor_copy(counts[:], misc[:, 0, 0:EXPERTS]))
            link(V.tensor_scalar(tiles[:], misc[:, 0, 0:EXPERTS], float(TILE - 1), None, ALU.add))
            link(V.tensor_single_scalar(tiles[:], tiles[:], TILE.bit_length() - 1, ALU.arith_shift_right))
            V.tensor_scalar(tiles[:], tiles[:], 1, None, ALU.max).then_inc(s["counted"], 1)
            dve.wait_ge(s["counted"], 1)

        @block.gpsimd
        def _(pool):
            G = nc.gpsimd
            alone = Alone(pool, "pool_awaited", (s["consts_made"], 2))

            def scale_of(b, name, stats_ready, mv_, rstd_, shift_, done):
                alone.wait_ge(s[stats_ready], b + 1)
                link = chain(alone, name, 3, b)
                link(G.tensor_scalar(rstd_[:], mv_[:, :, 1], EPS, None, ALU.add))
                link(G.tensor_tensor(rstd_[:], rstd_[:], minus_half[:], ALU.pow))
                link(G.tensor_tensor(shift_[:], mv_[:, :, 0], rstd_[:], ALU.mult))
                G.tensor_scalar(shift_[:], shift_[:], -1.0, None, ALU.mult).then_inc(s[done], 1)

            def scale_x(b):
                scale_of(b, "scale_chain", "ln_stats", mv, rstd, shift, "ln_scaled")

            def add_bias(b):
                pool.wait_ge(s["ln_done"], b * QT + QT)
                xb = x_all[:, bass.ds(b, 1)].rearrange("p o t d -> p (o t) d")
                G.tensor_tensor(xb, xb, bo_s[:].unsqueeze(1).to_broadcast([P, QT, D]), ALU.add).then_inc(s["bias_added"], 1)

            def split(b, what, use, units):
                alone.wait_ge(s["misc_read"], use.after(what))
                if not is_first(b):
                    alone.wait_ge(s["unit_written"], units)
                G.tensor_copy(high[what][:], dense[what][:]).then_inc(s["high_chain"], 1)
                alone.wait_ge(s["high_chain"], b * 2 + (1 if what == "K" else 2))
                G.tensor_tensor(rest[what][:], dense[what][:], high[what][:].bitcast(fp32),
                                ALU.subtract).then_inc(s["q_split" if what == "Q" else "k_split"], 1)

            def scatter(b):
                alone.wait_ge(s["rows_ready"], b + 1)
                for t in range(QT):
                    for c in range(2):
                        pool.indirect_dma_start(disp, bass.IndirectOffsetOnAxis(posi[:, c, t:t + 1], axis=0),
                                                row[:, t, :], None).then_inc(s["scattered"], 16)

            for n in range(3):
                load_third(pool, 0, n)
            pool.wait_ge(s["constants_ready"], 1)
            pool.wait_ge(s["consts_loaded"], 16 * NCONST)
            pool.wait_ge(s["consts_made"], 2)
            G.tensor_scalar(bo_s[:], bo_s[:], tg[:, 0:1], None, ALU.mult).then_inc(s["values_made"], 1)
            pool.wait_ge(s["values_made"], 1)
            for b, use in ((0, PRO0), (1, PRO1)):
                scale_x(b)
                split(b, "K", use, 4 * b - 2)
                split(b, "Q", use, 4 * b)
                add_bias(b)

            def body(b, par, use, ahead, nxt, back):
                if ahead:
                    scale_x(b + 2)
                    split(b + 2, "K", use, first_unit(b) - 2)
                if back:
                    scale_of(b - 1, "scale2_chain", "ln2_stats", mv2, rstd2, shift2, "ln2_scaled")
                if ahead:
                    split(b + 2, "Q", use, first_unit(b))
                    add_bias(b + 2)
                if back:
                    scatter(b - 1)

            over_batches(pool, body)
            scale_of(BATCHES - 1, "scale2_chain", "ln2_stats", mv2, rstd2, shift2, "ln2_scaled")
            scatter(BATCHES - 1)
            pool.wait_ge(s["scattered"], BATCHES * 16 * 2 * QT)


def expert_stage(nc, sb_in, sem, load_third, high_third, rest_third, disp, acc, idn, tiles, s_split, out):
    with ExitStack() as own:
        def sb(name, shape, dt=fp32):
            return sb_in(own, name, shape, dt)

        hi = [sb(f"w_hi{i}", [P, WCOLS], f32r) for i in range(2)]
        lo = [sb(f"w_lo{i}", [P, WCOLS], f32r) for i in range(2)]
        xg = sb("xg", [P, TT, ROW])
        x_hi = sb("x_hi", [P, HC, TILE], f32r)
        x_lo = sb("x_lo", [P, HC, TILE], f32r)
        silu = [sb(f"silu{i}", [P, 2, TILE]) for i in range(2)]
        h = [sb(f"h{i}", [P, 2, TILE]) for i in range(2)]
        h_hi = sb("h_hi", [P, IC, TILE], f32r)
        h_lo = sb("h_lo", [P, IC, TILE], f32r)
        weight = sb("weight", [P, TT])
        token = sb("token", [P, TT], i32)
        y = sb("y", [P, TT, D])
        noted_weight = sb("noted_weight", [P, TT])
        noted_token = sb("noted_token", [P, TT], i32)
        note = sb("note", [P, 4])

        turned = own.enter_context(nc.psum_tensor("turned", [P, HC, TILE], fp32))
        gate = [own.enter_context(nc.psum_tensor(f"gate{i}", [P, 2, TILE], fp32)) for i in range(2)]
        up = [own.enter_context(nc.psum_tensor(f"up{i}", [P, 2, TILE], fp32)) for i in range(2)]
        down = [own.enter_context(nc.psum_tensor(f"down{i}", [P, 512], fp32)) for i in range(TT)]

        s_rows = sem("rows_loaded")
        s_turned = sem("rows_turned")
        s_xhi = sem("x_hi_ready")
        s_xlo = sem("x_lo_ready")
        s_noted = sem("weights_and_tokens_noted")
        s_moved = sem("weights_and_tokens_moved")
        s_pair = sem("gate_up_written")
        s_silu = sem("silu_done")
        s_made = sem("gate_up_empty")
        s_hhi = sem("h_hi_ready")
        s_hlo = sem("h_lo_ready")
        s_down = sem("down_written")
        s_y = sem("down_read")
        s_added = sem("added")
        s_all = sem("all_added")
        s_out = sem("out_stored")

        def weights(par, which, mat):
            third = WCOLS // 3
            return which[par][:, mat * third:(mat + 1) * third].rearrange("p (c n) -> p c n", c=IC if mat == 2 else HC)

        def over_tiles(eng, name, tile, before_expert=None):
            n = eng.alloc_register(name)
            eng.reg_mov(n, 0)
            for e in range(EXPERTS):
                if before_expert:
                    before_expert(e)
                tile(e, 0, eng.snap(n), True)
                eng.reg_add(n, n, 1)
                count = eng.value_load(tiles[0:1, e:e + 1], min_val=1, max_val=TOKENS // TILE)
                with eng.If(count > 1):
                    with eng.Fori(1, count) as j:
                        tile(e, j, eng.snap(n), False)
                        eng.reg_add(n, n, 1)
            return eng.snap(n)

        block = own.enter_context(nc.Block())

        @block.sync
        def _(sp):
            def load_rows(first_row):
                sp.dma_start(xg[:], disp[bass.ds(first_row, TILE)].rearrange("(t p) d -> p t d", p=P)).then_inc(s_rows, 16)

            def tile(e, j, n, first):
                sp.wait_ge(s_noted, n)
                load_rows(j * TILE + e * REGION)

            total = over_tiles(sp, "sp_count", tile)
            sp.wait_ge(s_noted, total)
            load_rows(0)
            sp.wait_ge(s_all, 1)
            half = TOKENS // 2
            flat = out.rearrange("b s d -> (b s) d")
            sp.dma_start(flat[0:half], acc[0:half]).then_inc(s_out, 16)
            sp.wait_ge(s_out, 32)

        @block.tensor
        def _(pe):
            mm = nc.tensor.matmul

            def turn_rows(after_load):
                pe.wait_ge(s_rows, after_load)
                for t in range(TT):
                    for c in range(HC):
                        last = nc.tensor.transpose(turned[:, c, t * P:(t + 1) * P], xg[:, t, c * P:(c + 1) * P], idn[:])
                last.then_inc(s_turned, 1)

            def gate_up(par, pair, n):
                pe.wait_ge(s_made, n * PAIRS + (pair + 1))
                for mat, bank in ((0, gate[pair % 2]), (1, up[pair % 2])):
                    for i in range(2):
                        cols = slice((2 * pair + i) * P, (2 * pair + i + 1) * P)
                        terms = [(w, r, c) for w, r in ((hi, x_hi), (hi, x_lo), (lo, x_hi)) for c in range(HC)]
                        for m, (w, r, c) in enumerate(terms):
                            last = mm(bank[:, i, :], weights(par, w, mat)[:, c, cols], r[:, c, :],
                                      start=m == 0, stop=m == len(terms) - 1)
                last.then_inc(s_pair, 1)

            def contract(par, pair, n):
                pe.wait_ge(s_hlo, n * PAIRS + (pair + 1))
                if pair == 0:
                    pe.wait_ge(s_y, n * TT)
                for i in (2 * pair, 2 * pair + 1):
                    for t in range(TT):
                        for m, (r, w) in enumerate(((h_hi, hi), (h_lo, hi), (h_hi, lo))):
                            last = mm(down[t][:, 0:D], r[:, i, t * P:(t + 1) * P], weights(par, w, 2)[:, i, :],
                                      start=i == 0 and m == 0, stop=i == IC - 1 and m == 2)
                if pair == PAIRS - 1:
                    last.then_inc(s_down, 1)

            def tile(e, j, n, first):
                par = e % 2
                pe.wait_ge(s_xlo, n + 1)
                gate_up(par, 0, n)
                gate_up(par, 1, n)
                gate_up(par, 2, n)
                contract(par, 0, n)
                gate_up(par, 3, n)
                contract(par, 1, n)
                turn_rows(n * 16 + 32)
                contract(par, 2, n)
                contract(par, 3, n)

            turn_rows(16)
            over_tiles(pe, "pe_count", tile, lambda e: pe.wait_ge(s_split, 3 * (e + 1)))

        @block.scalar
        def _(act):
            def high_of_rows(done):
                act.wait_ge(s_turned, done)
                nc.scalar.activation(x_hi[:], turned[:], ACT.Copy).then_inc(s_xhi, 1)

            def tile(e, j, n, first):
                for pair in range(PAIRS):
                    act.wait_ge(s_pair, n * PAIRS + (pair + 1))
                    nc.scalar.activation(silu[pair % 2][:], gate[pair % 2][:], ACT.Silu).then_inc(s_silu, 1)
                    act.wait_ge(s_made, n * PAIRS + (pair + 3))
                    nc.scalar.activation(h_hi[:, 2 * pair:2 * pair + 2, :], h[pair % 2][:], ACT.Copy).then_inc(s_hhi, 1)
                    if first and e + 1 < EXPERTS and pair < 3:
                        high_third(act, e + 1, pair, hi[(e + 1) % 2])
                high_of_rows(n + 2)

            for n in range(3):
                high_third(act, 0, n, hi[0])
            high_of_rows(1)
            over_tiles(act, "act_count", tile)
            act.wait_ge(s_all, 1)
            half = TOKENS // 2
            act.dma_start(out.rearrange("b s d -> (b s) d")[half:], acc[half:TOKENS]).then_inc(s_out, 16)

        @block.vector
        def _(dve):
            V = nc.vector

            def rest_of_rows(done):
                dve.wait_ge(s_xhi, done)
                V.tensor_tensor(x_lo[:], turned[:], x_hi[:].bitcast(fp32), ALU.subtract).then_inc(s_xlo, 1)

            def tile(e, j, n, first):
                V.tensor_copy(noted_token[:], xg[:, :, TOKCOL].bitcast(i32))
                V.tensor_copy(noted_weight[:], xg[:, :, COMB + e]).then_inc(s_noted, 1)
                for pair in range(PAIRS):
                    dve.wait_ge(s_silu, n * PAIRS + (pair + 1))
                    V.tensor_tensor(h[pair % 2][:], silu[pair % 2][:], up[pair % 2][:], ALU.mult).then_inc(s_made, 1)
                    dve.wait_ge(s_hhi, n * PAIRS + (pair + 1))
                    V.tensor_tensor(h_lo[:, 2 * pair:2 * pair + 2, :], h[pair % 2][:],
                                    h_hi[:, 2 * pair:2 * pair + 2, :].bitcast(fp32), ALU.subtract).then_inc(s_hlo, 1)
                    if first and e + 1 < EXPERTS and pair < 3:
                        rest_third(dve, e + 1, pair, hi[(e + 1) % 2], lo[(e + 1) % 2])
                dve.wait_ge(s_noted, n + 1)
                dve.wait_ge(s_added, n * (16 * TT))
                V.tensor_copy(token[:], noted_token[:])
                V.tensor_copy(weight[:], noted_weight[:]).then_inc(s_moved, 1)
                rest_of_rows(n + 2)
                dve.wait_ge(s_moved, n + 1)
                dve.wait_ge(s_down, n + 1)
                for t in range(TT):
                    V.tensor_scalar(y[:, t, :], down[t][:, 0:D], weight[:, t:t + 1], None, ALU.mult).then_inc(s_y, 1)

            V.memset(note[:], 0.0).then_inc(s_made, 2)
            for n in range(3):
                rest_third(dve, 0, n, hi[0], lo[0])
            rest_of_rows(1)
            over_tiles(dve, "dve_count", tile)

        @block.gpsimd
        def _(pool):
            pool.wait_ge(s_split, 1)
            alone = Alone(pool, "pool_awaited2", (s_split, 1))

            def tile(e, j, n, first):
                for t in range(TT):
                    pool.wait_ge(s_y, n * TT + (t + 1))
                    alone.wait_ge(s_added, n * (16 * TT) + 16 * t)
                    pool.indirect_dma_start(acc, bass.IndirectOffsetOnAxis(token[:, t:t + 1], axis=0),
                                            y[:, t, :], None, compute_op=ALU.add).then_inc(s_added, 16)

            def load_weights(e):
                if e + 2 < EXPERTS:
                    for third in range(3):
                        pool.wait_ge(s_split, 3 * (e + 1) + third + 1)
                        load_third(pool, e + 2, third)

            load_weights(-1)
            total = over_tiles(pool, "pool_count", tile, load_weights)
            alone.wait_ge(s_added, total * (16 * TT))
            nc.gpsimd.memset(note[:, 0:1], 0.0).then_inc(s_all, 1)


def kernel(x, ctx_1024, g_xattn, g_ffn, L0_xattn_w_q, L0_xattn_b_q, L0_xattn_w_k, L0_xattn_b_k,
           L0_xattn_w_v, L0_xattn_b_v, L0_xattn_w_o, L0_xattn_b_o, L0_ffn_conf_w, L0_ffn_conf_b,
           L0_ffn_gate_w, L0_ffn_up_w, L0_ffn_down_w, L0_ffn_wealth):
    import numpy as np
    import concourse.bacc as bacc
    from concourse.bass_utils import run_bass_kernel_spmd

    def a(value):
        return np.asarray(value)

    blocks = P // DK
    heads = [HPP * (blocks // HPP * c + i % (blocks // HPP)) + i // (blocks // HPP) for c in range(HC) for i in range(blocks)]

    def head_columns(w):
        return np.ascontiguousarray(w.reshape(HEADS, DK, D)[heads].reshape(D, D).T)

    def head_rows(b):
        return np.ascontiguousarray(b.reshape(HEADS, DK)[heads].reshape(HC, P).T)

    def on_partitions(row, repeat=1):
        return np.ascontiguousarray(np.broadcast_to(np.tile(row.reshape(-1), repeat), (P, row.size * repeat)))

    pad_rows = np.zeros((P, ROW), np.float32)
    pad_rows[:, TOKCOL] = np.arange(TOKENS, TOKENS + P, dtype=np.int32).view(np.float32)
    pick_rows = np.zeros((P, 2, 2, BLOCKS, P), np.float32)
    for n, terms in enumerate((((0, 2), (1,)), ((0, 1), (2,)))):
        for part in range(2):
            for i in range(BLOCKS):
                for u in range(HPP):
                    for term in terms[part]:
                        for dim in range(DK):
                            pick_rows[DK * (BLOCKS * u + i) + dim, n, part, i, STACK * u + DK * term + dim] = 1
    ones_at = np.zeros((P, 1), np.float32)
    ones_at[SHIFT::STACK] = 1
    experts = np.arange(EXPERTS, dtype=np.float32)
    arrays = {
        "x": a(x),
        "ctxT": np.ascontiguousarray(a(ctx_1024).transpose(0, 2, 1)),
        "wq": head_columns(a(L0_xattn_w_q)),
        "wk": head_columns(a(L0_xattn_w_k)),
        "wv": np.ascontiguousarray(a(L0_xattn_w_v).T),
        "wo": np.ascontiguousarray(a(L0_xattn_w_o).T),
        "bq": head_rows(a(L0_xattn_b_q)),
        "bk": head_rows(a(L0_xattn_b_k)),
        "bv": on_partitions(a(L0_xattn_b_v)),
        "bo": on_partitions(a(L0_xattn_b_o)),
        "confT": np.ascontiguousarray(a(L0_ffn_conf_w).T),
        "conf_b": on_partitions(a(L0_ffn_conf_b), QT),
        "wealth": on_partitions(a(L0_ffn_wealth), QT),
        "g_attn": on_partitions(a(g_xattn)),
        "g_ffn": on_partitions(a(g_ffn)),
        "gate_T": np.ascontiguousarray(a(L0_ffn_gate_w).transpose(0, 2, 1)),
        "up_T": np.ascontiguousarray(a(L0_ffn_up_w).transpose(0, 2, 1)),
        "down_T": np.ascontiguousarray(a(L0_ffn_down_w).transpose(0, 2, 1)),
        "ident": np.eye(P, dtype=np.float32),
        "tri": np.triu(np.ones((P, P), np.float32), 1),
        "expert_row": on_partitions(experts * REGION, QT),
        "expert_no": on_partitions(experts, QT),
        "token_no": np.ascontiguousarray(np.arange(TOKENS, dtype=np.int32).reshape(-1, P).T),
        "ones_at": ones_at,
        "pick_rows": pick_rows.reshape(P, HPG, QT, SEQ),
        "pad_rows": pad_rows,
    }
    nc = bacc.Bacc("TRN2", target_bir_lowering=False, num_devices=1)
    handles = {name: nc.dram_tensor(name, list(v.shape), mybir.dt.from_np(v.dtype), kind="ExternalInput").ap()
               for name, v in arrays.items()}
    out = nc.dram_tensor("out", [BATCHES, SEQ, D], fp32, kind="ExternalOutput").ap()
    build_program(nc, out=out, **handles)
    result = run_bass_kernel_spmd(nc, [arrays], core_ids=[0])
    return result.results[0]["out"]
```

```python
import concourse.bass as bass
from concourse import mybir
from contextlib import ExitStack

BATCHES, SEQ, D = 16, 256, 256
HEADS, DK = 16, 16
EXPERTS, INNER = 8, 1024
P = 128
TOKENS = BATCHES * SEQ
HC = D // P
QT = SEQ // P
SLOT = 32
GROUPS = HEADS * SLOT // P
HPG = P // SLOT
STACK = 64
HPP = P // STACK
HPAIRS = HEADS // HPP
SHIFT = 3 * DK
TILE = 256
TT = TILE // P
REGION = TOKENS + TILE
ROW = 272
COMB = D
TOKCOL = D + EXPERTS
NFIRST, NCONST = 6, 13
BLOCKS = P // DK // HPP
MISC = 3
IC = INNER // P
PAIRS = IC // 2
WCOLS = 3 * HC * INNER
EPS = 1e-5
FAR = -3.0e38

fp32 = mybir.dt.float32
f32r = mybir.dt.float32r
i32 = mybir.dt.int32
ALU = mybir.AluOpType
ACT = mybir.ActivationFunctionType
AX = mybir.AxisListType


def build_program(nc, x, ctxT, wq, wk, wv, wo, bq, bk, bv, bo, confT, conf_b, wealth, g_attn, g_ffn,
                  gate_T, up_T, down_T, ident, tri, expert_row, expert_no, token_no, ones_at, pick_rows, pad_rows, out):
    disp = nc.dram_tensor("dispatched", [EXPERTS * REGION, ROW], fp32, kind="Internal").ap()

    with ExitStack() as keep:
        def sb(stack, name, shape, dt=fp32):
            return stack.enter_context(nc.sbuf_tensor(name, shape, dt))

        def sem(name):
            return keep.enter_context(nc.semaphore(name))

        stage = sb(keep, "stage", [P, WCOLS])
        idn = sb(keep, "idn", [P, P])
        pads = sb(keep, "pads", [P, ROW])
        counts = sb(keep, "counts", [P, EXPERTS], i32)
        tiles = sb(keep, "tiles", [P, EXPERTS], i32)

        s_stage = [sem(f"stage_loaded{n}") for n in range(3)]
        s_split = [sem(f"weights_split{n}") for n in range(3)]
        s_hi = sem("weights_hi")
        s_padded = [sem("expert0_padded"), sem("others_padded")]

        third = WCOLS // 3

        def load_third(eng, e, n):
            of = (gate_T, up_T, down_T)[n][e].rearrange("(c p) n -> p c n", p=P)
            eng.dma_start(stage[:, n * third:(n + 1) * third].rearrange("p (c n) -> p c n", c=of.shape[1]),
                          of).then_inc(s_stage[n], 16)

        def part(n, half):
            start = n * third + half * (third // 2)
            return slice(start, start + third // 2)

        ROUNDED = [(1, 0), (0, 0), (1, 1), (0, 1), (2, 0), (2, 1)]

        def round_weights(act, e, n, half, hi):
            act.wait_ge(s_stage[n], 16 * (e + 1))
            nc.scalar.activation(hi[:, part(n, half)], stage[:, part(n, half)], ACT.Copy).then_inc(s_hi, 1)

        def rest_of_weights(eng, e, n, half, hi, lo):
            eng.wait_ge(s_hi, len(ROUNDED) * e + ROUNDED.index((n, half)) + 1)
            eng.tensor_tensor(lo[:, part(n, half)], stage[:, part(n, half)], hi[:, part(n, half)].bitcast(fp32),
                              ALU.subtract).then_inc(s_split[n], 1)

        attention_stage(nc, sb, sem, load_third, disp, out, x, ctxT, wq, wk, wv, wo,
                        bq, bk, bv, bo, confT, conf_b, wealth, g_attn, g_ffn, ident, tri,
                        expert_row, expert_no, token_no, ones_at, pick_rows, pad_rows, idn, pads, s_padded, counts, tiles)
        expert_stage(nc, sb, sem, load_third, round_weights, rest_of_weights, disp, out, idn, tiles,
                     s_split, s_padded, ROUNDED)


class Alone:

    def __init__(self, eng, name, seen):
        self.eng, self.seen, self.register = eng, seen, eng.alloc_register(name)

    def wait_ge(self, semaphore, value):
        if not isinstance(value, int):
            self.eng.reg_mov(self.register, value)
            value = self.register
        self.eng.wait_ge(*self.seen)
        self.eng.wait_ge(semaphore, value)


def attention_stage(nc, sb_in, sem, load_third, disp, out, x, ctxT, wq, wk, wv, wo,
                    bq, bk, bv, bo, confT, conf_b, wealth, g_attn, g_ffn, ident, tri,
                    expert_row, expert_no, token_no, ones_at, pick_rows, pad_rows, idn, pads, s_padded, counts, tiles):
    with ExitStack() as own:
        def sb(name, shape, dt=fp32):
            return sb_in(own, name, shape, dt)

        x_all = sb("x_all", [P, BATCHES, QT, D])
        cT = [sb(f"ctxT{i}", [P, HC, SEQ]) for i in range(2)]
        wq_s = sb("wq_s", [P, HC, D])
        wk_s = sb("wk_s", [P, HC, D])
        wv_s = sb("wv_s", [P, HC, D])
        wo_s = sb("wo_s", [P, HC, D])
        bq_s = sb("bq_s", [P, HC])
        bk_s = sb("bk_s", [P, HC])
        bv_s = sb("bv_s", [P, D])
        bo_s = sb("bo_s", [P, D])
        conf_s = sb("conf_s", [P, HC, EXPERTS])
        cb_s = sb("cb_s", [P, QT, EXPERTS])
        wealth_s = sb("wealth_s", [P, QT, EXPERTS])
        eoff = sb("eoff", [P, QT, EXPERTS])
        eno = sb("eno", [P, QT, EXPERTS])
        tok = sb("tok", [P, BATCHES * QT], i32)
        tri_s = sb("tri_s", [P, P])
        before = sb("before", [P, P], f32r)
        ones = sb("ones", [P, P], f32r)
        gates = sb("gates", [P, 2])
        tg = sb("tg", [P, 2])
        minus_half = sb("minus_half", [P, QT])
        stats = sb("stats", [P, QT, 6])
        mv = sb("mv", [P, QT, 2])
        rstd = sb("rstd", [P, QT])
        shift = sb("shift", [P, QT])
        stats2 = sb("stats2", [P, QT, 6])
        mv2 = sb("mv2", [P, QT, 2])
        rstd2 = sb("rstd2", [P, QT])
        shift2 = sb("shift2", [P, QT])
        xn = sb("xn", [P, QT, D])
        xT = sb("xT", [P, HC, SEQ])
        dense = {what: sb(f"{what}_dense", [P, HC, SEQ]) for what in "QK"}
        high = {what: sb(f"{what}_high", [P, HC, SEQ], f32r) for what in "QK"}
        rest = {what: sb(f"{what}_rest", [P, HC, SEQ], f32r) for what in "QK"}
        q = [sb(f"queries{i}", [P, HPAIRS, SEQ], f32r) for i in range(2)]
        k = [sb(f"keys{i}", [P, HPAIRS, SEQ], f32r) for i in range(2)]
        picks = {what: sb(f"picks_{what}", [P, BLOCKS, P], f32r) for what in ("Q high", "Q rest", "K high", "K rest")}
        ones_row = sb("ones_row", [P, 1])
        max_neg = sb("max_neg", [P, QT, HEADS])
        max_rows = sb("max_rows", [HEADS, SEQ], f32r)
        v = [sb(f"values{i}", [P, QT, HEADS, SLOT]) for i in range(2)]
        probs = [sb(f"probs{i}", [P, HPG, QT, SEQ]) for i in range(2)]
        oS = sb("oS", [P, GROUPS, SEQ])
        rsum = sb("rsum", [P, QT, HEADS])
        on = sb("on", [P, QT, D])
        oT = sb("oT", [P, HC, SEQ])
        row = [sb(f"row{i}", [P, QT, ROW]) for i in range(2)]
        x2T = sb("x2T", [P, HC, SEQ])
        z = sb("z", [P, QT, EXPERTS])
        ez = sb("ez", [P, QT, EXPERTS])
        bids = sb("bids", [P, QT, EXPERTS])
        t8 = sb("t8", [P, QT, EXPERTS])
        u8 = sb("u8", [P, QT, EXPERTS])
        bqs = sb("bqs", [P, HC])
        m1 = sb("m1", [P, QT, EXPERTS])
        m2 = sb("m2", [P, QT, EXPERTS])
        m12 = sb("m12", [P, QT, EXPERTS], f32r)
        macc = sb("macc", [P, EXPERTS], f32r)
        v1 = sb("v1", [P, QT])
        v2 = sb("v2", [P, QT])
        r1 = sb("r1", [P, QT])
        dv = sb("dv", [P, QT])
        ed = sb("ed", [P, QT])
        w1 = sb("w1", [P, QT])
        s8 = sb("s8", [P, QT, EXPERTS])
        sum2 = sb("sum2", [P, QT])
        c8 = sb("c8", [P, QT, EXPERTS])
        w2 = sb("w2", [P, QT])
        posf = sb("posf", [P, 2, QT])
        posi = sb("posi", [P, 2, QT], i32)

        scores = own.enter_context(nc.psum_tensor("scores", [P, HPP * QT, SEQ], fp32))
        maxps = own.enter_context(nc.psum_tensor("maxps", [P, 2, QT, SEQ], fp32))
        pv = own.enter_context(nc.psum_tensor("pv", [P, 512], fp32))
        misc = own.enter_context(nc.psum_tensor("misc", [P, MISC, 2, 256], fp32))


        names = """x_loaded x_rest_loaded ctx_loaded consts_loaded pads_loaded pads_stored consts_made constants_ready
            misc_written ln_stats ln_chain ln_scaled ln_done ln2_chain ln2_stats ln2_scaled
            ln2_done bias_added q_split k_split high_chain unit_written unit_read first_loaded picks_loaded picks_ready half_made shifted max_scored max_taken pv_done pv_read
            sums_inverted x2_stored sigmoid_half_ready route_chain masks_ready second_ready
            rows_chain rows_ready scattered count_chain counted values_made
            scale_chain scale2_chain""".split()
        s = {n: sem(n) for n in names}
        misc_read = [sem(f"misc_read{n}") for n in range(MISC)]

        AHEAD, NEXT, LATE = ["K", "TX", "Q"], ["V", "MT"], ["RK"]
        BACK = ["TO0", "TO1", "TN", "WO", "TX2", "LG"]
        FULL = ["V", "TO0", "TO1", "K", "TX", "TN", "WO", "RK", "Q", "TX2", "MT", "LG"]

        class Use:

            def __init__(self, order, before, rounds=None):
                self.order, self.before = order, before
                self.phase, self.rounds = (before % MISC, before // MISC) if rounds is None else (0, rounds)

            def place(self, what):
                n = self.phase + self.order.index(what)
                return n % MISC, self.rounds + n // MISC

            def bank(self, what):
                return misc[:, self.place(what)[0]]

            def freed(self, what):
                return misc_read[self.place(what)[0]]

            def free(self, eng, what):
                n, uses = self.place(what)
                if not (isinstance(uses, int) and uses == 0):
                    eng.wait_ge(misc_read[n], uses)

            def written(self, eng, what):
                eng.wait_ge(s["misc_written"], self.before + (self.order.index(what) + 1))

            def read(self, eng, what):
                n, uses = self.place(what)
                eng.wait_ge(misc_read[n], uses + 1)

        UNITS = ["S0", "S1", "S2", "S3", "S4", "K0", "S5", "S6", "S7", "K1", "Q0", "Q1"]
        STACKS = ["K0", "K1", "Q0", "Q1"]

        def units_before(b):
            last = isinstance(b, int) and b == BATCHES - 1
            return b * len(UNITS) + (2 * len(STACKS) if not last else len(STACKS))

        def unit(b, what):
            order = [n for n in UNITS if n not in STACKS] if isinstance(b, int) and b >= BATCHES - 2 else UNITS
            return units_before(b) + order.index(what)

        def first_stack_unit(b, what):
            return b * len(STACKS) + STACKS.index(what)

        def after_all(use):
            return use.before + len(use.order)

        PRO0 = Use(["TX", "K", "Q"], 0)
        PRO1 = Use(["V", "TX", "K", "Q", "MT"], after_all(PRO0))

        def without(*parts):
            return [n for n in FULL if not any(n in part for part in parts)]

        ITER0 = Use(without(BACK, LATE), after_all(PRO1))
        ITER1 = Use(without(LATE), after_all(ITER0))
        before2 = after_all(ITER1)
        assert before2 % MISC == 0 and len(FULL) % MISC == 0

        def full_use(b):
            rounds = len(FULL) // MISC
            return Use(FULL, b * len(FULL) + (before2 - 2 * len(FULL)), b * rounds + (before2 // MISC - 2 * rounds))

        ITER14 = Use(without(AHEAD), after_all(full_use(BATCHES - 3)))
        ITER15 = Use(without(AHEAD, NEXT), after_all(ITER14))
        EPILOGUE = Use(without(AHEAD, NEXT), after_all(ITER15))
        EPILOGUE2 = Use(LATE + ["COUNT"], after_all(EPILOGUE))

        def over_batches(eng, body):
            body(0, 0, ITER0, True, True, False, False)
            body(1, 1, ITER1, True, True, True, False)
            with eng.Fori(1, BATCHES // 2 - 1) as i:
                for b, par in ((i * 2, 0), (i * 2 + 1, 1)):
                    body(b, par, full_use(b), True, True, True, True)
            body(BATCHES - 2, 0, ITER14, False, True, True, True)
            body(BATCHES - 1, 1, ITER15, False, False, True, True)

        def of_batch(b, t):
            return x_all[:, bass.ds(b, 1), t, :].rearrange("p o d -> p (o d)")

        def is_first(b):
            return isinstance(b, int) and b == 0

        def chain(eng, name, each, b, behind=0, start=0):
            n = [start]

            def link(instruction):
                n[0] += 1
                assert n[0] <= each
                instruction.then_inc(s[name], 1)
                if n[0] - start > behind:
                    eng.wait_ge(s[name], b * each + n[0] - behind)
            return link

        def pad_experts(eng, experts):
            eng.wait_ge(s["pads_loaded"], 16)
            eng.wait_ge(s["counted"], 1)
            for e in experts:
                n = eng.value_load(counts[0:1, e:e + 1], min_val=0, max_val=TOKENS)
                eng.dma_start(disp[bass.ds(n + e * REGION, TILE)].rearrange("(t p) d -> p t d", p=P),
                              pads[:].unsqueeze(1).to_broadcast([P, TT, ROW])).then_inc(s_padded[min(e, 1)], 16)

        block = own.enter_context(nc.Block())

        @block.sync
        def _(sp):
            def load_x(b, loaded="x_loaded"):
                sp.dma_start(x_all[:, b], x[b].rearrange("(t p) d -> p t d", p=P)).then_inc(s[loaded], 16)

            def load(of_all, name):
                for to, of in of_all:
                    sp.dma_start(to, of).then_inc(s[name], 16)

            def load_ctx(b, par):
                if not is_first(b):
                    sp.wait_ge(s["ctx_loaded"], b * 16)
                sp.dma_start(cT[par][:], ctxT[bass.ds(b, 1)].rearrange("o (c p) s -> p (o c) s", p=P)).then_inc(s["ctx_loaded"], 16)

            load_x(0)
            first = ((idn[:], ident), (wk_s[:], wk.rearrange("(c p) n -> p c n", p=P)), (bk_s[:], bk),
                     (wq_s[:], wq.rearrange("(c p) n -> p c n", p=P)), (bq_s[:], bq), (ones_row[:], ones_at))
            assert len(first) == NFIRST
            load(first[:1], "first_loaded")
            load_ctx(0, 0)
            load(first[1:], "first_loaded")
            load(((probs[0][:], pick_rows),), "picks_loaded")
            load_ctx(1, 1)
            sp.wait_ge(s["x_loaded"], 16)
            load_x(1)
            consts = ((wv_s[:], wv.rearrange("(c p) n -> p c n", p=P)), (bv_s[:], bv),
                      (gates[:, 0:1], g_attn), (gates[:, 1:2], g_ffn), (bo_s[:], bo),
                      (wo_s[:], wo.rearrange("(c p) n -> p c n", p=P)),
                      (conf_s[:], confT.rearrange("(c p) n -> p c n", p=P)), (cb_s[:], conf_b),
                      (wealth_s[:], wealth), (eoff[:], expert_row), (eno[:], expert_no),
                      (tri_s[:], tri), (tok[:], token_no))
            assert len(consts) == NCONST
            load(consts, "consts_loaded")
            load(((pads[:], pad_rows),), "pads_loaded")

            def store_shift(b, par, use):
                use.read(sp, "MT")
                for u in range(HPP):
                    row_ = u * STACK + SHIFT
                    sp.dma_start(q[par][row_:row_ + 1].bitcast(fp32), max_rows[u * HPAIRS:(u + 1) * HPAIRS].bitcast(fp32)).then_inc(s["shifted"], 16)

            for b in range(2, BATCHES):
                load_x(b, "x_rest_loaded")
            store_shift(0, 0, PRO1)
            sp.wait_ge(s["pads_loaded"], 16)
            sp.dma_start(out[TOKENS:], pads[:, 0:D]).then_inc(s["pads_stored"], 16)

            def store_residual(b, use):
                use.read(sp, "WO")
                sp.dma_start(out[bass.ds(b * SEQ, SEQ)].rearrange("(t p) d -> p t d", p=P),
                             x_all[:, bass.ds(b, 1)].rearrange("p o t d -> p (o t) d")).then_inc(s["x2_stored"], 16)

            def body(b, par, use, ahead, nxt, back, late):
                if ahead:
                    sp.wait_ge(s["misc_written"], use.before)
                    load_ctx(b + 2, par)
                if back:
                    store_residual(b - 1, use)
                if nxt:
                    store_shift(b + 1, 1 - par, use)

            over_batches(sp, body)
            store_residual(BATCHES - 1, EPILOGUE)
            pad_experts(sp, range(0, EXPERTS, 2))
            sp.wait_ge(s["x2_stored"], 16 * BATCHES)
            sp.wait_ge(s["pads_stored"], 16)

        @block.tensor
        def _(pe):
            mm = nc.tensor.matmul

            def turn(source, what, use):
                use.free(pe, what)
                for t in range(QT):
                    for c in range(HC):
                        last = nc.tensor.transpose(use.bank(what)[:, c, t * P:(t + 1) * P], source[:, t, c * P:(c + 1) * P], idn[:])
                last.then_inc(s["misc_written"], 1)

            def turn_x(b, use):
                pe.wait_ge(s["ln_done"], b * QT + QT)
                turn(xn, "TX", use)

            def project(weights, source, what, use):
                use.free(pe, what)
                for o in range(HC):
                    for c in range(HC):
                        last = mm(use.bank(what)[:, o, :], weights[:, c, o * P:(o + 1) * P], source[:, c, :], start=c == 0, stop=c == HC - 1)
                last.then_inc(s["misc_written"], 1)

            def project_q(use):
                use.read(pe, "TX")
                project(wq_s, xT, "Q", use)

            def project_k(b, par, use):
                pe.wait_ge(s["ctx_loaded"], b * 16 + 16)
                project(wk_s, cT[par], "K", use)

            def project_v(par, use):
                use.free(pe, "V")
                for t in range(QT):
                    for c in range(HC):
                        last = mm(use.bank("V")[:, t, :], cT[par][:, c, t * P:(t + 1) * P], wv_s[:, c, :], start=c == 0, stop=c == HC - 1)
                last.then_inc(s["misc_written"], 1)

            def write_unit(n):
                if not (isinstance(n, int) and n == 0):
                    pe.wait_ge(s["unit_read"], n)

            def stack(b, what, c, n):
                if c == 0:
                    pe.wait_ge(s["q_split" if what == "Q" else "k_split"], b + 1)
                write_unit(n)
                for i in range(BLOCKS):
                    mm(scores[:, i, :], picks[what + " high"][:, i, :], high[what][:, c, :], start=True, stop=False)
                    last = mm(scores[:, i, :], picks[what + " rest"][:, i, :], rest[what][:, c, :], start=False, stop=True)
                last.then_inc(s["unit_written"], 1)

            def max_scores(b, par, pair, units):
                if pair == 0:
                    pe.wait_ge(s["unit_read"], units)
                if not (is_first(b) and pair == 0):
                    pe.wait_ge(s["max_taken"], b * HPAIRS + pair)
                for t in range(QT):
                    for u in range(HPP):
                        r = slice(u * STACK, u * STACK + SHIFT)
                        last = mm(maxps[:, u, t, :], q[par][r, pair, t * P:(t + 1) * P], k[par][r, pair, :], start=True, stop=True)
                last.then_inc(s["max_scored"], 1)

            def turn_maxima(b, use):
                pe.wait_ge(s["max_taken"], b * HPAIRS + HPAIRS)
                use.free(pe, "MT")
                for t in range(QT):
                    last = nc.tensor.transpose(use.bank("MT")[0:HEADS, 0, t * P:(t + 1) * P], max_neg[:, t, :], idn[:])
                last.then_inc(s["misc_written"], 1)

            def score(b, par, pair):
                if pair == 0:
                    pe.wait_ge(s["shifted"], b * (16 * HPP) + 16 * HPP)
                write_unit(unit(b, f"S{pair}"))
                for t in range(QT):
                    for u in range(HPP):
                        r = slice(u * STACK, (u + 1) * STACK)
                        last = mm(scores[:, u * QT + t, :], k[par][r, pair, t * P:(t + 1) * P], q[par][r, pair, :],
                                  start=True, stop=True)
                last.then_inc(s["unit_written"], 1)

            def weigh(b, par, g):
                pe.wait_ge(s["unit_read"], unit(b, f"S{2 * g + 1}") + 1)
                if not (is_first(b) and g == 0):
                    pe.wait_ge(s["pv_read"], b * GROUPS + g)
                for t in range(QT):
                    for j in range(HPG):
                        last = mm(pv[j * SLOT:(j + 1) * SLOT, 0:SEQ], v[par][:, t, g * HPG + j, :], probs[g % 2][:, j, t, :],
                                  start=t == 0, stop=t == QT - 1)
                last.then_inc(s["pv_done"], 1)

            def turn_heads(b, t, use):
                if t == 0:
                    pe.wait_ge(s["pv_read"], b * GROUPS + GROUPS)
                use.free(pe, f"TO{t}")
                for g in range(GROUPS):
                    last = nc.tensor.transpose(use.bank(f"TO{t}")[:, g // 2, (g % 2) * P:(g % 2 + 1) * P], oS[:, g, t * P:(t + 1) * P], idn[:])
                last.then_inc(s["misc_written"], 1)

            def turn_normed(use):
                use.read(pe, "TO1")
                turn(on, "TN", use)

            def attn_out(use):
                use.read(pe, "TN")
                use.free(pe, "WO")
                for t in range(QT):
                    for c in range(HC):
                        last = mm(use.bank("WO")[:, t, :], oT[:, c, t * P:(t + 1) * P], wo_s[:, c, :], start=c == 0, stop=c == HC - 1)
                last.then_inc(s["misc_written"], 1)

            def turn_x2(b, par, use):
                pe.wait_ge(s["ln2_done"], b * QT + QT)
                turn(row[par], "TX2", use)

            def logits(use):
                use.read(pe, "TX2")
                use.free(pe, "LG")
                for t in range(QT):
                    for c in range(HC):
                        last = mm(use.bank("LG")[:, t, 0:EXPERTS], x2T[:, c, t * P:(t + 1) * P], conf_s[:, c, :], start=c == 0, stop=c == HC - 1)
                last.then_inc(s["misc_written"], 1)

            def ranks(b, use):
                pe.wait_ge(s["masks_ready"], b + 1)
                use.free(pe, "RK")
                for t in range(QT):
                    mm(use.bank("RK")[:, t, 0:EXPERTS], before[:], m12[:, t, :], start=True, stop=False)
                    if t == 1:
                        mm(use.bank("RK")[:, t, 0:EXPERTS], ones[:], m12[:, 0, :], start=False, stop=False)
                    last = mm(use.bank("RK")[:, t, 0:EXPERTS], ones[:], macc[:], start=False, stop=True)
                last.then_inc(s["misc_written"], 1)

            pe.wait_ge(s["first_loaded"], 16 * NFIRST)
            turn_x(0, PRO0)
            project_k(0, 0, PRO0)
            project_q(PRO0)
            pe.wait_ge(s["picks_ready"], 1)

            def stack_first(b, what):
                stack(b, what[0], int(what[1]), first_stack_unit(b, what))

            for what in STACKS:
                stack_first(0, what)
            pe.wait_ge(s["consts_loaded"], 16 * NCONST)
            pe.wait_ge(s["constants_ready"], 1)
            project_v(0, PRO1)
            turn_x(1, PRO1)
            max_scores(0, 0, 0, len(STACKS))
            project_k(1, 1, PRO1)
            max_scores(0, 0, 1, len(STACKS))
            project_q(PRO1)
            for pair in range(2, HPAIRS):
                max_scores(0, 0, pair, len(STACKS))
                if pair < 6:
                    stack_first(1, STACKS[pair - 2])
            turn_maxima(0, PRO1)

            def body(b, par, use, ahead, nxt, back, late):
                def max_of_next(pair):
                    if nxt:
                        max_scores(b + 1, 1 - par, pair, units_before(b))

                def stack_ahead(what):
                    if ahead:
                        stack(b + 2, what[0], int(what[1]), unit(b, what))

                if nxt:
                    project_v(1 - par, use)
                max_of_next(0)
                if back:
                    turn_heads(b - 1, 0, use)
                score(b, par, 0)
                if back:
                    turn_heads(b - 1, 1, use)
                max_of_next(1)
                if ahead:
                    project_k(b + 2, par, use)
                score(b, par, 1)
                max_of_next(2)
                if ahead:
                    turn_x(b + 2, use)
                if back:
                    turn_normed(use)
                score(b, par, 2)
                weigh(b, par, 0)
                score(b, par, 3)
                max_of_next(3)
                if back:
                    attn_out(use)
                score(b, par, 4)
                max_of_next(4)
                if late:
                    ranks(b - 2, use)
                stack_ahead("K0")
                weigh(b, par, 1)
                score(b, par, 5)
                if ahead:
                    project_q(use)
                max_of_next(5)
                score(b, par, 6)
                weigh(b, par, 2)
                max_of_next(6)
                score(b, par, 7)
                if back:
                    turn_x2(b - 1, 1 - par, use)
                max_of_next(7)
                stack_ahead("K1")
                weigh(b, par, 3)
                if nxt:
                    turn_maxima(b + 1, use)
                stack_ahead("Q0")
                if back:
                    logits(use)
                stack_ahead("Q1")

            over_batches(pe, body)
            last_batch = BATCHES - 1
            turn_heads(last_batch, 0, EPILOGUE)
            turn_heads(last_batch, 1, EPILOGUE)
            turn_normed(EPILOGUE)
            attn_out(EPILOGUE)
            ranks(last_batch - 1, EPILOGUE)
            turn_x2(last_batch, last_batch % 2, EPILOGUE)
            logits(EPILOGUE)
            ranks(last_batch, EPILOGUE2)
            pe.wait_ge(s["rows_ready"], BATCHES)
            EPILOGUE2.free(pe, "COUNT")
            mm(EPILOGUE2.bank("COUNT")[:, 0, 0:EXPERTS], ones[:], macc[:], start=True, stop=True).then_inc(s["misc_written"], 1)

        @block.scalar
        def _(act):
            def exps(b, pair):
                act.wait_ge(s["unit_written"], unit(b, f"S{pair}") + 1)
                g = pair // 2
                if not (is_first(b) and g < 2):
                    act.wait_ge(s["pv_done"], b * GROUPS + (g - 1))
                at = pair % 2 * HPP
                nc.scalar.activation(probs[g % 2][:, at:at + HPP].rearrange("p u t s -> p (u t) s"), scores[:],
                                     ACT.Exp).then_inc(s["unit_read"], 1)

            def read_stack(par, what, c, n):
                to, bias = (q, 0.0) if what == "Q" else (k, ones_row[:, 0:1])
                act.wait_ge(s["unit_written"], n + 1)
                nc.scalar.activation(to[par][:, c * BLOCKS:(c + 1) * BLOCKS, :], scores[:], ACT.Identity,
                                     bias=bias).then_inc(s["unit_read"], 1)

            def norm_x(b):
                act.wait_ge(s["ln_scaled"], b + 1)
                for t in range(QT):
                    nc.scalar.activation(xn[:, t, :], of_batch(b, t), ACT.Identity,
                                         bias=shift[:, t:t + 1], scale=rstd[:, t:t + 1]).then_inc(s["ln_done"], 1)

            def norm_x2(b, par):
                act.wait_ge(s["ln2_scaled"], b + 1)
                if not (isinstance(b, int) and b < 2):
                    act.wait_ge(s["scattered"], (b - 1) * (16 * 2 * QT))
                for t in range(QT):
                    nc.scalar.activation(row[par][:, t, 0:D], of_batch(b, t), ACT.Identity, bias=shift2[:, t:t + 1],
                                         scale=rstd2[:, t:t + 1]).then_inc(s["ln2_done"], 1)

            def read_whole(to, what, use):
                use.written(act, what)
                nc.scalar.activation(to, use.bank(what)[:], ACT.Copy).then_inc(use.freed(what), 1)

            def read_dense(b, what, bias, scale, use):
                use.written(act, what)
                if not is_first(b):
                    act.wait_ge(s["q_split" if what == "Q" else "k_split"], b)
                for c in range(HC):
                    last = nc.scalar.activation(dense[what][:, c, :], use.bank(what)[:, c, :], ACT.Identity, bias=bias[:, c:c + 1], scale=scale)
                last.then_inc(use.freed(what), 1)

            def read_q(b, use):
                read_dense(b, "Q", bqs, DK ** -0.5, use)

            def read_k(b, use):
                read_dense(b, "K", bk_s, 1.0, use)

            def read_pv(b, g):
                act.wait_ge(s["pv_done"], b * GROUPS + (g + 1))
                nc.scalar.activation(oS[:, g, :], pv[:, 0:SEQ], ACT.Copy).then_inc(s["pv_read"], 1)

            def sigmoid(use):
                use.read(act, "LG")
                nc.scalar.activation(ez[:], z[:], ACT.Exp, scale=-1.0).then_inc(s["sigmoid_half_ready"], 1)

            def second_weight(b):
                act.wait_ge(s["masks_ready"], b + 1)
                nc.scalar.activation(ed[:], dv[:], ACT.Exp).then_inc(s["second_ready"], 1)

            def high_part(b, what, use):
                use.read(act, what)
                if not is_first(b):
                    act.wait_ge(s["unit_written"], first_stack_unit(b - 1, what + "1") + 1)
                nc.scalar.activation(high[what][:], dense[what][:], ACT.Copy).then_inc(s["high_chain"], 1)

            act.wait_ge(s["first_loaded"], 16 * NFIRST)
            nc.scalar.activation(bqs[:], bq_s[:], ACT.Copy, scale=DK ** -0.5).then_inc(s["consts_made"], 1)
            act.wait_ge(s["consts_made"], 1)
            for b, use in ((0, PRO0), (1, PRO1)):
                norm_x(b)
                read_whole(xT[:], "TX", use)
                read_k(b, use)
                high_part(b, "K", use)
                read_q(b, use)
                high_part(b, "Q", use)
                for what in STACKS:
                    read_stack(b, what[0], int(what[1]), first_stack_unit(b, what))
                if b == 0:
                    act.wait_ge(s["consts_loaded"], 16 * NCONST)
                    nc.scalar.activation(tg[:], gates[:], ACT.Tanh).then_inc(s["consts_made"], 1)

            def body(b, par, use, ahead, nxt, back, late):
                def stack_ahead(what):
                    if ahead:
                        read_stack(par, what[0], int(what[1]), unit(b, what))

                if ahead:
                    norm_x(b + 2)
                exps(b, 0)
                exps(b, 1)
                if ahead:
                    read_k(b + 2, use)
                    read_whole(xT[:], "TX", use)
                exps(b, 2)
                if back:
                    read_whole(oT[:], "TN", use)
                read_pv(b, 0)
                exps(b, 3)
                exps(b, 4)
                if late:
                    second_weight(b - 2)
                stack_ahead("K0")
                read_pv(b, 1)
                exps(b, 5)
                if ahead:
                    read_q(b + 2, use)
                exps(b, 6)
                if back:
                    norm_x2(b - 1, 1 - par)
                read_pv(b, 2)
                exps(b, 7)
                if back:
                    read_whole(x2T[:], "TX2", use)
                stack_ahead("K1")
                read_pv(b, 3)
                stack_ahead("Q0")
                if back:
                    sigmoid(use)
                stack_ahead("Q1")

            over_batches(act, body)
            read_whole(oT[:], "TN", EPILOGUE)
            second_weight(BATCHES - 2)
            norm_x2(BATCHES - 1, (BATCHES - 1) % 2)
            read_whole(x2T[:], "TX2", EPILOGUE)
            sigmoid(EPILOGUE)
            second_weight(BATCHES - 1)
            pad_experts(act, range(1, EXPERTS, 2))

        @block.vector
        def _(dve):
            V = nc.vector
            alone = Alone(dve, "dve_awaited", (s["x_loaded"], 16))
            both8 = [P, QT, EXPERTS]

            def spread(column):
                return column[:].unsqueeze(2).to_broadcast(both8)

            def stats_x(b):
                if isinstance(b, int) and b < 2:
                    dve.wait_ge(s["x_loaded"], b * 16 + 16)
                else:
                    dve.wait_ge(s["x_rest_loaded"], 16 * (BATCHES - 2))
                if not is_first(b):
                    alone.wait_ge(s["ln_stats"], b)
                link = chain(alone, "ln_chain", QT, b)
                for t in range(QT):
                    link(V.bn_stats(stats[:, t, :], of_batch(b, t)))
                if not is_first(b):
                    alone.wait_ge(s["ln_done"], b * QT)
                for t in range(QT):
                    last = V.bn_aggr(mv[:, t, :], stats[:, t, :])
                last.then_inc(s["ln_stats"], 1)

            def norm_heads(b, t, use):
                use.written(dve, f"TO{t}")
                heads = use.bank(f"TO{t}")[:].rearrange("p a (h c) -> p (a h) c", c=SLOT)
                V.reciprocal(rsum[:, t, :], heads[:, :, DK]).then_inc(s["sums_inverted"], 1)
                dve.wait_ge(s["sums_inverted"], b * QT + (t + 1))
                V.tensor_tensor(on[:, t, :].rearrange("p (h d) -> p h d", d=DK), heads[:, :, 0:DK],
                                rsum[:, t, :].unsqueeze(2).to_broadcast([P, HEADS, DK]), ALU.mult).then_inc(use.freed(f"TO{t}"), 1)

            def residual(b, use):
                use.written(dve, "WO")
                dve.wait_ge(s["bias_added"], b + 1)
                if not is_first(b):
                    dve.wait_ge(s["ln2_done"], b * QT)
                xb = x_all[:, bass.ds(b, 1)].rearrange("p o t d -> p (o t d)")
                V.scalar_tensor_tensor(xb, use.bank("WO")[:].rearrange("p t d -> p (t d)"), tg[:, 0:1], xb,
                                       ALU.mult, ALU.add).then_inc(use.freed("WO"), 1)
                use.read(alone, "WO")
                link = chain(alone, "ln2_chain", QT, b)
                for t in range(QT):
                    link(V.bn_stats(stats2[:, t, :], of_batch(b, t)))
                for t in range(QT):
                    last = V.bn_aggr(mv2[:, t, :], stats2[:, t, :])
                last.then_inc(s["ln2_stats"], 1)

            def read_v(par, use):
                use.written(dve, "V")
                for t in range(QT):
                    last = V.tensor_tensor(v[par][:, t, :, 0:DK], use.bank("V")[:, t, :].rearrange("p (h d) -> p h d", d=DK),
                                           bv_s[:].rearrange("p (h d) -> p h d", d=DK), ALU.add)
                last.then_inc(use.freed("V"), 1)

            def maxima(b, pair):
                dve.wait_ge(s["max_scored"], b * HPAIRS + (pair + 1))
                to = max_neg[:].rearrange("p t (u n) -> p u t n", u=HPP)[:, :, :, pair]
                V.tensor_reduce(to, maxps[:], AX.X, ALU.max, negate=True).then_inc(s["max_taken"], 1)

            def read_maxima(b, use):
                use.written(dve, "MT")
                if not is_first(b):
                    dve.wait_ge(s["shifted"], b * (16 * HPP))
                V.tensor_copy(max_rows[:], use.bank("MT")[0:HEADS, 0, :]).then_inc(use.freed("MT"), 1)

            def read_logits(b, use):
                use.written(dve, "LG")
                V.tensor_tensor(z[:], use.bank("LG")[:, :, 0:EXPERTS], cb_s[:], ALU.add).then_inc(use.freed("LG"), 1)

            def first_choice(b):
                dve.wait_ge(s["sigmoid_half_ready"], b + 1)
                link = chain(dve, "route_chain", 14, b)
                link(V.tensor_scalar(t8[:], ez[:], 1.0, None, ALU.add))
                link(V.reciprocal(u8[:], t8[:]))
                link(V.tensor_tensor(bids[:], u8[:], wealth_s[:], ALU.mult))
                link(V.tensor_reduce(v1[:], bids[:], AX.X, ALU.max))
                link(V.tensor_tensor(t8[:], bids[:], spread(v1), ALU.is_equal))
                link(V.scalar_tensor_tensor(u8[:], t8[:], -float(EXPERTS), eno[:], ALU.mult, ALU.add))
                link(V.tensor_reduce(r1[:], u8[:], AX.X, ALU.min))
                link(V.tensor_tensor(m1[:], u8[:], spread(r1), ALU.is_equal))

            def second_choice(b):
                link = chain(dve, "route_chain", 14, b, start=8)
                link(V.scalar_tensor_tensor(bids[:], m1[:], FAR, bids[:], ALU.mult, ALU.add))
                link(V.tensor_reduce(v2[:], bids[:], AX.X, ALU.max))
                V.tensor_tensor(dv[:], v2[:], v1[:], ALU.subtract)
                link(V.tensor_tensor(t8[:], bids[:], spread(v2), ALU.is_equal))
                link(V.scalar_tensor_tensor(u8[:], t8[:], -float(EXPERTS), eno[:], ALU.mult, ALU.add))
                link(V.tensor_reduce(r1[:], u8[:], AX.X, ALU.min))
                link(V.tensor_tensor(m2[:], u8[:], spread(r1), ALU.is_equal))
                V.tensor_tensor(m12[:], m1[:], m2[:], ALU.add).then_inc(s["masks_ready"], 1)

            def positions(b, par, use):
                use.written(dve, "RK")
                if not is_first(b):
                    dve.wait_ge(s["scattered"], b * (16 * 2 * QT))
                V.tensor_tensor(u8[:], use.bank("RK")[:, :, 0:EXPERTS], eoff[:], ALU.add).then_inc(use.freed("RK"), 1)
                use.read(dve, "RK")
                dve.wait_ge(s["second_ready"], b + 1)
                link = chain(dve, "rows_chain", 14, b, behind=1)
                link(V.tensor_tensor(t8[:], m1[:], u8[:], ALU.mult))
                link(V.tensor_tensor(s8[:], m2[:], u8[:], ALU.mult))
                link(V.tensor_reduce(posf[:, 0, :], t8[:], AX.X, ALU.add))
                link(V.tensor_reduce(posf[:, 1, :], s8[:], AX.X, ALU.add))
                link(V.tensor_scalar(sum2[:], ed[:], 1.0, None, ALU.add))
                link(V.tensor_copy(posi[:], posf[:]))
                link(V.reciprocal(v1[:], sum2[:]))
                link(V.tensor_copy(row[par][:, :, TOKCOL:TOKCOL + 1].bitcast(i32),
                                   tok[:, bass.ds(b * QT, QT)].unsqueeze(2)))
                link(V.tensor_scalar(w1[:], v1[:], tg[:, 1:2], None, ALU.mult))
                link(V.tensor_tensor(macc[:], macc[:].bitcast(fp32), m12[:, 0, :].bitcast(fp32), ALU.add))
                link(V.tensor_tensor(w2[:], w1[:], ed[:], ALU.mult))
                link(V.tensor_tensor(macc[:], macc[:].bitcast(fp32), m12[:, 1, :].bitcast(fp32), ALU.add))
                link(V.tensor_tensor(t8[:], m1[:], spread(w1), ALU.mult))
                link(V.tensor_tensor(c8[:], m2[:], spread(w2), ALU.mult))
                dve.wait_ge(s["rows_chain"], b * 14 + 14)
                V.tensor_tensor(row[par][:, :, COMB:COMB + EXPERTS], t8[:], c8[:], ALU.add).then_inc(s["rows_ready"], 1)

            def rest_part(b, what):
                dve.wait_ge(s["high_chain"], b * 2 + (1 if what == "K" else 2))
                V.tensor_tensor(rest[what][:], dense[what][:], high[what][:].bitcast(fp32),
                                ALU.subtract).then_inc(s["q_split" if what == "Q" else "k_split"], 1)

            stats_x(0)
            dve.wait_ge(s["picks_loaded"], 16)
            loaded = probs[0][:].rearrange("p m t (h c) -> p m (t h) c", c=P)
            for n, what in enumerate("QK"):
                for m, part in enumerate(("high", "rest")):
                    last = V.tensor_copy(picks[f"{what} {part}"][:], loaded[:, 2 * n + m])
            last.then_inc(s["picks_ready"], 1)
            stats_x(1)
            V.memset(v[0][:], 1.0)
            V.memset(v[1][:], 1.0)
            V.memset(macc[:].bitcast(fp32), 0.0)
            rest_part(0, "K")
            for rows in row:
                V.memset(rows[:, :, D:], 0.0)
            rest_part(0, "Q")
            V.memset(ones[:].bitcast(fp32), 1.0).then_inc(s["constants_ready"], 1)
            dve.wait_ge(s["constants_ready"], 1)
            dve.wait_ge(s["consts_loaded"], 16 * NCONST)
            dve.wait_ge(s["consts_made"], 2)
            V.tensor_copy(before[:], tri_s[:])
            read_v(0, PRO1)
            for pair in range(HPAIRS):
                maxima(0, pair)
                if pair == 1:
                    rest_part(1, "K")
                if pair == 2:
                    rest_part(1, "Q")
            read_maxima(0, PRO1)

            def body(b, par, use, ahead, nxt, back, late):
                def max_of_next(pair):
                    if nxt:
                        maxima(b + 1, pair)

                if ahead:
                    stats_x(b + 2)
                if nxt:
                    read_v(1 - par, use)
                max_of_next(0)
                if back:
                    norm_heads(b - 1, 0, use)
                max_of_next(1)
                if back:
                    norm_heads(b - 1, 1, use)
                max_of_next(2)
                if late:
                    first_choice(b - 2)
                max_of_next(3)
                if late:
                    second_choice(b - 2)
                if back:
                    residual(b - 1, use)
                max_of_next(4)
                if late:
                    positions(b - 2, par, use)
                max_of_next(5)
                max_of_next(6)
                max_of_next(7)
                if nxt:
                    read_maxima(b + 1, use)
                if back:
                    read_logits(b - 1, use)

            over_batches(dve, body)
            b = BATCHES - 1
            norm_heads(b, 0, EPILOGUE)
            norm_heads(b, 1, EPILOGUE)
            first_choice(b - 1)
            second_choice(b - 1)
            residual(b, EPILOGUE)
            positions(b - 1, 1 - b % 2, EPILOGUE)
            read_logits(b, EPILOGUE)
            first_choice(b)
            second_choice(b)
            positions(b, b % 2, EPILOGUE2)
            EPILOGUE2.written(dve, "COUNT")
            link = chain(dve, "count_chain", 4, 0)
            link(V.tensor_copy(counts[:], EPILOGUE2.bank("COUNT")[:, 0, 0:EXPERTS]))
            link(V.tensor_scalar(tiles[:], EPILOGUE2.bank("COUNT")[:, 0, 0:EXPERTS], float(TILE - 1), None, ALU.add))
            link(V.tensor_single_scalar(tiles[:], tiles[:], TILE.bit_length() - 1, ALU.arith_shift_right))
            V.tensor_scalar(tiles[:], tiles[:], 1, None, ALU.max).then_inc(s["counted"], 1)
            dve.wait_ge(s["counted"], 1)

        @block.gpsimd
        def _(pool):
            G = nc.gpsimd
            alone = Alone(pool, "pool_awaited", (s["half_made"], 1))

            def scale_of(b, name, stats_ready, mv_, rstd_, shift_, done):
                alone.wait_ge(s[stats_ready], b + 1)
                link = chain(alone, name, 3, b)
                link(G.tensor_scalar(rstd_[:], mv_[:, :, 1], EPS, None, ALU.add))
                link(G.tensor_tensor(rstd_[:], rstd_[:], minus_half[:], ALU.pow))
                link(G.tensor_tensor(shift_[:], mv_[:, :, 0], rstd_[:], ALU.mult))
                G.tensor_scalar(shift_[:], shift_[:], -1.0, None, ALU.mult).then_inc(s[done], 1)

            def scale_x(b):
                scale_of(b, "scale_chain", "ln_stats", mv, rstd, shift, "ln_scaled")

            def add_bias(b):
                pool.wait_ge(s["ln_done"], b * QT + QT)
                xb = x_all[:, bass.ds(b, 1)].rearrange("p o t d -> p (o t) d")
                G.tensor_tensor(xb, xb, bo_s[:].unsqueeze(1).to_broadcast([P, QT, D]), ALU.add).then_inc(s["bias_added"], 1)

            def split(b, what, use, units):
                use.read(alone, what)
                if not is_first(b):
                    alone.wait_ge(s["unit_written"], units)
                G.tensor_copy(high[what][:], dense[what][:]).then_inc(s["high_chain"], 1)
                alone.wait_ge(s["high_chain"], b * 2 + (1 if what == "K" else 2))
                G.tensor_tensor(rest[what][:], dense[what][:], high[what][:].bitcast(fp32),
                                ALU.subtract).then_inc(s["q_split" if what == "Q" else "k_split"], 1)

            def scatter(b, par):
                alone.wait_ge(s["rows_ready"], b + 1)
                for t in range(QT):
                    for c in range(2):
                        pool.indirect_dma_start(disp, bass.IndirectOffsetOnAxis(posi[:, c, t:t + 1], axis=0),
                                                row[par][:, t, :], None).then_inc(s["scattered"], 16)

            G.memset(minus_half[:], -0.5).then_inc(s["half_made"], 1)
            pool.wait_ge(s["half_made"], 1)
            scale_x(0)
            for n in range(3):
                load_third(pool, 0, n)
            scale_x(1)
            pool.wait_ge(s["consts_loaded"], 16 * NCONST)
            pool.wait_ge(s["consts_made"], 2)
            G.tensor_scalar(bo_s[:], bo_s[:], tg[:, 0:1], None, ALU.mult).then_inc(s["values_made"], 1)
            pool.wait_ge(s["values_made"], 1)
            add_bias(0)
            add_bias(1)

            def body(b, par, use, ahead, nxt, back, late):
                if ahead:
                    scale_x(b + 2)
                    split(b + 2, "K", use, units_before(b) + (UNITS.index("K1") + 1 - len(UNITS)))
                if back:
                    scale_of(b - 1, "scale2_chain", "ln2_stats", mv2, rstd2, shift2, "ln2_scaled")
                if ahead:
                    split(b + 2, "Q", use, units_before(b))
                if late:
                    scatter(b - 2, par)
                if ahead:
                    add_bias(b + 2)

            over_batches(pool, body)
            scale_of(BATCHES - 1, "scale2_chain", "ln2_stats", mv2, rstd2, shift2, "ln2_scaled")
            scatter(BATCHES - 2, BATCHES % 2)
            scatter(BATCHES - 1, (BATCHES - 1) % 2)
            pool.wait_ge(s["scattered"], BATCHES * 16 * 2 * QT)


def expert_stage(nc, sb_in, sem, load_third, round_weights, rest_of_weights, disp, out, idn, tiles, s_split, s_padded, ROUNDED):
    with ExitStack() as own:
        def sb(name, shape, dt=fp32):
            return sb_in(own, name, shape, dt)

        hi = [sb(f"w_hi{i}", [P, WCOLS], f32r) for i in range(2)]
        lo = [sb(f"w_lo{i}", [P, WCOLS], f32r) for i in range(2)]
        xg = sb("xg", [P, TT, ROW])
        x_hi = sb("x_hi", [P, HC, TILE], f32r)
        x_lo = sb("x_lo", [P, HC, TILE], f32r)
        silu = [sb(f"silu{i}", [P, 2, TILE]) for i in range(2)]
        h = [sb(f"h{i}", [P, 2, TILE]) for i in range(2)]
        h_hi = sb("h_hi", [P, IC, TILE], f32r)
        h_lo = sb("h_lo", [P, IC, TILE], f32r)
        weight = sb("weight", [P, TT])
        token = sb("token", [P, TT], i32)
        y = sb("y", [P, TT, D])
        noted_weight = sb("noted_weight", [P, TT])
        noted_token = sb("noted_token", [P, TT], i32)
        note = sb("note", [P, 4])

        turned = own.enter_context(nc.psum_tensor("turned", [P, HC, TILE], fp32))
        gate = [own.enter_context(nc.psum_tensor(f"gate{i}", [P, 2, TILE], fp32)) for i in range(2)]
        up = [own.enter_context(nc.psum_tensor(f"up{i}", [P, 2, TILE], fp32)) for i in range(2)]
        down = [own.enter_context(nc.psum_tensor(f"down{i}", [P, 512], fp32)) for i in range(TT)]

        s_rows = sem("rows_loaded")
        s_turned = sem("rows_turned")
        s_xhi = sem("x_hi_ready")
        s_xlo = sem("x_lo_ready")
        s_noted = sem("weights_and_tokens_noted")
        s_moved = sem("weights_and_tokens_moved")
        s_pair = sem("gate_up_written")
        s_silu = sem("silu_done")
        s_made = sem("gate_up_empty")
        s_hhi = sem("h_hi_ready")
        s_hlo = sem("h_lo_ready")
        s_down = sem("down_written")
        s_y = sem("down_read")
        s_added = sem("added")

        def weights(par, which, mat):
            third = WCOLS // 3
            return which[par][:, mat * third:(mat + 1) * third].rearrange("p (c n) -> p c n", c=IC if mat == 2 else HC)

        def over_tiles(eng, name, tile, before_expert=None):
            n = eng.alloc_register(name)
            eng.reg_mov(n, 0)
            for e in range(EXPERTS):
                if before_expert:
                    before_expert(e)
                tile(e, 0, eng.snap(n), True)
                eng.reg_add(n, n, 1)
                count = eng.value_load(tiles[0:1, e:e + 1], min_val=1, max_val=TOKENS // TILE)
                with eng.If(count > 1):
                    with eng.Fori(1, count) as j:
                        tile(e, j, eng.snap(n), False)
                        eng.reg_add(n, n, 1)
            return eng.snap(n)

        block = own.enter_context(nc.Block())

        @block.sync
        def _(sp):
            def load_rows(first_row):
                sp.dma_start(xg[:], disp[bass.ds(first_row, TILE)].rearrange("(t p) d -> p t d", p=P)).then_inc(s_rows, 16)

            def tile(e, j, n, first):
                sp.wait_ge(s_noted, n)
                if first and e < 2:
                    sp.wait_ge(s_padded[e], 16 if e == 0 else 16 * (EXPERTS - 1))
                load_rows(j * TILE + e * REGION)

            total = over_tiles(sp, "sp_count", tile)
            sp.wait_ge(s_noted, total)
            load_rows(0)

        @block.tensor
        def _(pe):
            mm = nc.tensor.matmul

            def turn_rows(after_load):
                pe.wait_ge(s_rows, after_load)
                for t in range(TT):
                    for c in range(HC):
                        last = nc.tensor.transpose(turned[:, c, t * P:(t + 1) * P], xg[:, t, c * P:(c + 1) * P], idn[:])
                last.then_inc(s_turned, 1)

            def gate_up(par, pair, n):
                pe.wait_ge(s_made, n * PAIRS + (pair + 1))
                for mat, bank in ((0, gate[pair % 2]), (1, up[pair % 2])):
                    for i in range(2):
                        cols = slice((2 * pair + i) * P, (2 * pair + i + 1) * P)
                        terms = [(w, r, c) for w, r in ((hi, x_hi), (hi, x_lo), (lo, x_hi)) for c in range(HC)]
                        for m, (w, r, c) in enumerate(terms):
                            last = mm(bank[:, i, :], weights(par, w, mat)[:, c, cols], r[:, c, :],
                                      start=m == 0, stop=m == len(terms) - 1)
                last.then_inc(s_pair, 1)

            def contract(e, pair, n, first):
                par = e % 2
                pe.wait_ge(s_hlo, n * PAIRS + (pair + 1))
                if pair == 0 and first:
                    pe.wait_ge(s_split[2], 2 * (e + 1))
                if pair == 0:
                    pe.wait_ge(s_y, n * TT)
                for i in (2 * pair, 2 * pair + 1):
                    for t in range(TT):
                        for m, (r, w) in enumerate(((h_hi, hi), (h_lo, hi), (h_hi, lo))):
                            last = mm(down[t][:, 0:D], r[:, i, t * P:(t + 1) * P], weights(par, w, 2)[:, i, :],
                                      start=i == 0 and m == 0, stop=i == IC - 1 and m == 2)
                if pair == PAIRS - 1:
                    last.then_inc(s_down, 1)

            def tile(e, j, n, first):
                par = e % 2
                pe.wait_ge(s_xlo, n + 1)
                gate_up(par, 0, n)
                gate_up(par, 1, n)
                gate_up(par, 2, n)
                contract(e, 0, n, first)
                gate_up(par, 3, n)
                contract(e, 1, n, first)
                turn_rows(n * 16 + 32)
                contract(e, 2, n, first)
                contract(e, 3, n, first)

            def gate_up_split(e):
                for n in range(2):
                    pe.wait_ge(s_split[n], 2 * (e + 1))

            turn_rows(16)
            over_tiles(pe, "pe_count", tile, gate_up_split)

        @block.scalar
        def _(act):
            def high_of_rows(done):
                act.wait_ge(s_turned, done)
                nc.scalar.activation(x_hi[:], turned[:], ACT.Copy).then_inc(s_xhi, 1)

            def tile(e, j, n, first):
                def next_weights(n, half):
                    if first and e + 1 < EXPERTS:
                        round_weights(act, e + 1, n, half, hi[(e + 1) % 2])

                for pair in range(PAIRS):
                    act.wait_ge(s_pair, n * PAIRS + (pair + 1))
                    nc.scalar.activation(silu[pair % 2][:], gate[pair % 2][:], ACT.Silu).then_inc(s_silu, 1)
                    next_weights(*((1, pair) if pair < 2 else (2, pair - 2)))
                    act.wait_ge(s_made, n * PAIRS + (pair + 3))
                    nc.scalar.activation(h_hi[:, 2 * pair:2 * pair + 2, :], h[pair % 2][:], ACT.Copy).then_inc(s_hhi, 1)
                    if pair < 2:
                        next_weights(0, pair)
                high_of_rows(n + 2)

            for n, half in ROUNDED[:4]:
                round_weights(act, 0, n, half, hi[0])
            high_of_rows(1)
            for n, half in ROUNDED[4:]:
                round_weights(act, 0, n, half, hi[0])
            over_tiles(act, "act_count", tile)

        @block.vector
        def _(dve):
            V = nc.vector

            def rest_of_rows(done):
                dve.wait_ge(s_xhi, done)
                V.tensor_tensor(x_lo[:], turned[:], x_hi[:].bitcast(fp32), ALU.subtract).then_inc(s_xlo, 1)

            def tile(e, j, n, first):
                V.tensor_copy(noted_token[:], xg[:, :, TOKCOL].bitcast(i32))
                V.tensor_copy(noted_weight[:], xg[:, :, COMB + e]).then_inc(s_noted, 1)
                for pair in range(PAIRS):
                    dve.wait_ge(s_silu, n * PAIRS + (pair + 1))
                    V.tensor_tensor(h[pair % 2][:], silu[pair % 2][:], up[pair % 2][:], ALU.mult).then_inc(s_made, 1)
                    dve.wait_ge(s_hhi, n * PAIRS + (pair + 1))
                    V.tensor_tensor(h_lo[:, 2 * pair:2 * pair + 2, :], h[pair % 2][:],
                                    h_hi[:, 2 * pair:2 * pair + 2, :].bitcast(fp32), ALU.subtract).then_inc(s_hlo, 1)
                    if first and e + 1 < EXPERTS:
                        rest_of_weights(dve, e + 1, 1 + pair // 2, pair % 2, hi[(e + 1) % 2], lo[(e + 1) % 2])
                dve.wait_ge(s_noted, n + 1)
                dve.wait_ge(s_added, n * (16 * TT))
                V.tensor_copy(token[:], noted_token[:])
                V.tensor_copy(weight[:], noted_weight[:]).then_inc(s_moved, 1)
                rest_of_rows(n + 2)
                dve.wait_ge(s_moved, n + 1)
                dve.wait_ge(s_down, n + 1)
                for t in range(TT):
                    V.tensor_scalar(y[:, t, :], down[t][:, 0:D], weight[:, t:t + 1], None, ALU.mult).then_inc(s_y, 1)

            V.memset(note[:], 0.0).then_inc(s_made, 2)
            for n, half in ((1, 0), (1, 1), (0, 1)):
                rest_of_weights(dve, 0, n, half, hi[0], lo[0])
            rest_of_rows(1)
            for half in range(2):
                rest_of_weights(dve, 0, 2, half, hi[0], lo[0])
            over_tiles(dve, "dve_count", tile)

        @block.gpsimd
        def _(pool):
            seen = (s_split[0], 2)
            alone = Alone(pool, "pool_awaited2", seen)

            def prepare_weights(e):
                for half in range(2 if e > 0 else 1):
                    rest_of_weights(pool, e, 0, half, hi[e % 2], lo[e % 2])
                if e + 1 < EXPERTS:
                    for n in range(3):
                        pool.wait_ge(s_split[n], 2 * (e + 1))
                        load_third(pool, e + 1, n)

            prepare_weights(0)

            def tile(e, j, n, first):
                if first and e + 1 < EXPERTS:
                    prepare_weights(e + 1)
                for t in range(TT):
                    pool.wait_ge(s_y, n * TT + (t + 1))
                    alone.wait_ge(s_added, n * (16 * TT) + 16 * t)
                    pool.indirect_dma_start(out, bass.IndirectOffsetOnAxis(token[:, t:t + 1], axis=0),
                                            y[:, t, :], None, compute_op=ALU.add).then_inc(s_added, 16)

            total = over_tiles(pool, "pool_count", tile)
            alone.wait_ge(s_added, total * (16 * TT))


def kernel(x, ctx_1024, g_xattn, g_ffn, L0_xattn_w_q, L0_xattn_b_q, L0_xattn_w_k, L0_xattn_b_k,
           L0_xattn_w_v, L0_xattn_b_v, L0_xattn_w_o, L0_xattn_b_o, L0_ffn_conf_w, L0_ffn_conf_b,
           L0_ffn_gate_w, L0_ffn_up_w, L0_ffn_down_w, L0_ffn_wealth):
    import numpy as np
    import concourse.bacc as bacc
    from concourse.bass_utils import run_bass_kernel_spmd

    def a(value):
        return np.asarray(value)

    blocks = P // DK
    heads = [HPP * (blocks // HPP * c + i % (blocks // HPP)) + i // (blocks // HPP) for c in range(HC) for i in range(blocks)]

    def head_columns(w):
        return np.ascontiguousarray(w.reshape(HEADS, DK, D)[heads].reshape(D, D).T)

    def head_rows(b):
        return np.ascontiguousarray(b.reshape(HEADS, DK)[heads].reshape(HC, P).T)

    def on_partitions(row, repeat=1):
        return np.ascontiguousarray(np.broadcast_to(np.tile(row.reshape(-1), repeat), (P, row.size * repeat)))

    pad_rows = np.zeros((P, ROW), np.float32)
    pad_rows[:, TOKCOL] = np.arange(TOKENS, TOKENS + P, dtype=np.int32).view(np.float32)
    pick_rows = np.zeros((P, 2, 2, BLOCKS, P), np.float32)
    for n, terms in enumerate((((0, 2), (1,)), ((0, 1), (2,)))):
        for part in range(2):
            for i in range(BLOCKS):
                for u in range(HPP):
                    for term in terms[part]:
                        for dim in range(DK):
                            pick_rows[DK * (BLOCKS * u + i) + dim, n, part, i, STACK * u + DK * term + dim] = 1
    ones_at = np.zeros((P, 1), np.float32)
    ones_at[SHIFT::STACK] = 1
    experts = np.arange(EXPERTS, dtype=np.float32)
    arrays = {
        "x": a(x),
        "ctxT": np.ascontiguousarray(a(ctx_1024).transpose(0, 2, 1)),
        "wq": head_columns(a(L0_xattn_w_q)),
        "wk": head_columns(a(L0_xattn_w_k)),
        "wv": np.ascontiguousarray(a(L0_xattn_w_v).T),
        "wo": np.ascontiguousarray(a(L0_xattn_w_o).T),
        "bq": head_rows(a(L0_xattn_b_q)),
        "bk": head_rows(a(L0_xattn_b_k)),
        "bv": on_partitions(a(L0_xattn_b_v)),
        "bo": on_partitions(a(L0_xattn_b_o)),
        "confT": np.ascontiguousarray(a(L0_ffn_conf_w).T),
        "conf_b": on_partitions(a(L0_ffn_conf_b), QT),
        "wealth": on_partitions(a(L0_ffn_wealth), QT),
        "g_attn": on_partitions(a(g_xattn)),
        "g_ffn": on_partitions(a(g_ffn)),
        "gate_T": np.ascontiguousarray(a(L0_ffn_gate_w).transpose(0, 2, 1)),
        "up_T": np.ascontiguousarray(a(L0_ffn_up_w).transpose(0, 2, 1)),
        "down_T": np.ascontiguousarray(a(L0_ffn_down_w).transpose(0, 2, 1)),
        "ident": np.eye(P, dtype=np.float32),
        "tri": np.triu(np.ones((P, P), np.float32), 1),
        "expert_row": on_partitions(experts * REGION, QT),
        "expert_no": on_partitions(experts, QT),
        "token_no": np.ascontiguousarray(np.arange(TOKENS, dtype=np.int32).reshape(-1, P).T),
        "ones_at": ones_at,
        "pick_rows": pick_rows.reshape(P, HPG, QT, SEQ),
        "pad_rows": pad_rows,
    }
    nc = bacc.Bacc("TRN2", target_bir_lowering=False, num_devices=1)
    handles = {name: nc.dram_tensor(name, list(v.shape), mybir.dt.from_np(v.dtype), kind="ExternalInput").ap()
               for name, v in arrays.items()}
    out = nc.dram_tensor("out", [TOKENS + P, D], fp32, kind="ExternalOutput").ap()
    build_program(nc, out=out, **handles)
    result = run_bass_kernel_spmd(nc, [arrays], core_ids=[0])
    return result.results[0]["out"][:TOKENS].reshape(BATCHES, SEQ, D)
```
